# Optimizing a Trainium2 kernel written in Bass

```python
import numpy as np
import jax
import jax.numpy as jnp

def _softmax(x, axis=-1):
    return jax.nn.softmax(x, axis=axis)

def _gelu(x):
    return jax.nn.gelu(x, approximate=True)

def _silu(x):
    return jax.nn.silu(x)

def _sigmoid(x):
    return jax.nn.sigmoid(x)

def _layernorm(x, axis=-1, eps=1e-05):
    m = jnp.mean(x, axis=axis, keepdims=True)
    v = jnp.var(x, axis=axis, keepdims=True)
    return (x - m) / jnp.sqrt(v + eps)

def _scatter_add(tgt, idx, src, axis=0):
    return tgt.at[idx].add(src)

def _segment_sum(src, seg, n):
    return jax.ops.segment_sum(src, seg, n)
kernel_name = 'mk_adj_preln_d2_adj_r2_c60171'

def setup_inputs(seed: int=0):
    np.random.seed(seed)
    _w = jnp.asarray

    def _rec_inputs():
        import jax
        import jax.numpy as jnp
        _gk = jax.random.key(seed)
        x = -0.000929 + 1 * jax.random.normal(jax.random.fold_in(_gk, 1), (8192, 128), jnp.float32)
        _a = jax.random.bernoulli(jax.random.fold_in(_gk, 2), 0.000976562, (8192, 8192))
        adj = _a.astype(jnp.int32)
        return (x, adj)
    x, adj = _rec_inputs()

    def _L0_gnn_setup():
        import jax, jax.numpy as jnp
        import numpy as np
        NEG_INF = -9000000000000000.0
        ALPHA = 0.2
        key = jax.random.key(seed)
        k1, k2, k3, k4 = jax.random.split(key, 4)
        N, F_in, F_out = (4096, 128, 128)
        x = jax.random.normal(k1, (N, F_in), dtype=jnp.float32)
        adj = jax.random.randint(k2, (N, N), 0, 2, dtype=jnp.int32)
        W = jax.random.normal(k3, (F_in, F_out), dtype=jnp.float32) * (1.0 / np.sqrt(F_in))
        a = jax.random.normal(k4, (2 * F_out, 1), dtype=jnp.float32) * (1.0 / np.sqrt(2 * F_out))
        return {'x': x, 'adj': adj, 'W': W, 'a': a}
    _L0_gnn_all = _L0_gnn_setup()
    _L0_gnn_in = {k: v for k, v in _L0_gnn_all.items() if k in ('W', 'a')}
    del _L0_gnn_all

    def _L1_gnn_setup():
        import jax, jax.numpy as jnp
        import numpy as np
        ALPHA = 0.2
        NEG_BIG = -9000000000000000.0
        key = jax.random.key(seed)
        k1, k2, k3, k4 = jax.random.split(key, 4)
        N, F_IN, F_OUT = (4096, 128, 128)
        h = jax.random.normal(k1, (N, F_IN), dtype=jnp.float32)
        adj = jax.random.randint(k2, (N, N), 0, 2, dtype=jnp.int32)
        W = jax.random.normal(k3, (F_IN, F_OUT), dtype=jnp.float32) * (1.0 / np.sqrt(F_IN))
        a = jax.random.normal(k4, (2 * F_OUT, 1), dtype=jnp.float32) * (1.0 / np.sqrt(2 * F_OUT))
        return {'h': h, 'adj': adj, 'W': W, 'a': a}
    _L1_gnn_all = _L1_gnn_setup()
    _L1_gnn_in = {k: v for k, v in _L1_gnn_all.items() if k in ('W', 'a')}
    del _L1_gnn_all
    return {'x': x, 'adj': adj, 'L0_gnn_W': _L0_gnn_in['W'], 'L0_gnn_a': _L0_gnn_in['a'], 'L1_gnn_W': _L1_gnn_in['W'], 'L1_gnn_a': _L1_gnn_in['a']}

def reference(x, adj, L0_gnn_W, L0_gnn_a, L1_gnn_W, L1_gnn_a):
    import jax
    import jax.numpy as jnp

    def _L0_gnn_ref(x, adj, W, a):
        import jax, jax.numpy as jnp
        import numpy as np
        NEG_INF = -9000000000000000.0
        ALPHA = 0.2
        h = x @ W
        F_out = h.shape[1]
        a_src = a[:F_out, 0]
        a_dst = a[F_out:, 0]
        s_src = h @ a_src
        s_dst = h @ a_dst
        e = jax.nn.leaky_relu(s_src[:, None] + s_dst[None, :], negative_slope=ALPHA)
        e = jnp.where(adj > 0, e, jnp.float32(NEG_INF))
        attention = jax.nn.softmax(e, axis=1)
        h_prime = attention @ h
        return h_prime

    def _L1_gnn_ref(h, adj, W, a):
        import jax, jax.numpy as jnp
        import numpy as np
        ALPHA = 0.2
        NEG_BIG = -9000000000000000.0
        Wh = h @ W
        F_out = Wh.shape[1]
        a1 = a[:F_out, 0]
        a2 = a[F_out:, 0]
        e = (Wh @ a1)[:, None] + (Wh @ a2)[None, :]
        e = jnp.where(e >= 0, e, ALPHA * e)
        scores = jnp.where(adj > 0, e, NEG_BIG)
        attention = jax.nn.softmax(scores, axis=1)
        return attention @ Wh
    h = jnp.maximum(_layernorm(x, axis=-1), 0.0)
    x = x + _L0_gnn_ref(h, adj, L0_gnn_W, L0_gnn_a)
    h = jnp.maximum(_layernorm(x, axis=-1), 0.0)
    x = x + _L1_gnn_ref(h, adj, L1_gnn_W, L1_gnn_a)
    return x

_drawn_inputs = setup_inputs


def setup_inputs(seed=0):
    import zlib

    import numpy as np

    out = dict(_drawn_inputs(seed))
    spreads = {}
    factors = {}
    for name, (base, spread) in spreads.items():
        noise = np.random.default_rng([zlib.crc32(name.encode()), seed]).standard_normal(out[name].shape)
        drawn = base * np.exp(spread * noise) if base else spread * noise
        out[name] = jnp.asarray(drawn.astype(out[name].dtype))
    for name, factor in factors.items():
        out[name] = (out[name] * factor).astype(out[name].dtype)
    return out
```

```python
from contextlib import ExitStack

import concourse.bass as bass
from concourse import mybir

P = 128
ALU = mybir.AluOpType
ACT = mybir.ActivationFunctionType
F32 = mybir.dt.float32
F16 = mybir.dt.float16
BF16 = mybir.dt.bfloat16
I32 = mybir.dt.int32
AX_X = mybir.AxisListType.X
RMAX = bass.bass_isa.ReduceOp.max
RADD = bass.bass_isa.ReduceOp.add

SLOPE = 0.2
LN_EPS = 1e-5
STEEP = 2.0 ** 100
EXPONENT_BITS = 0x7F800000
ONE_SQUARED_BITS = float(0x7F000000)
LEAST_NORMAL_BITS = float(0x00800000)
FP16_ROOM = 2500.0

RING = 4
JG = 2
IB = 8
QUAD = 4


def gat2_kernel(nc, x, adj, W, WT, a, out):
    N, F = x.shape
    LAYERS = W.shape[0]
    T = N // P
    CHUNKS = T // IB
    CW = IB * P
    GROUPS = T // JG
    ROUNDS = GROUPS // RING
    QUADS = T // QUAD
    FD = F + 1
    DVE_STEPS = 14
    assert F == P and T % IB == 0 and GROUPS % RING == 0 and ROUNDS >= 3 and QUADS % 2 == 0

    x_tiles = x.rearrange("(t p) f -> p t f", p=P)
    out_tiles = out.rearrange("(t p) f -> p t f", p=P)

    with ExitStack() as ctx:
        def sb(name, shape, dt=F32):
            return ctx.enter_context(nc.sbuf_tensor(name, shape, dt))

        def sem(name):
            return ctx.enter_context(nc.semaphore(name))

        X = sb("X", [P, T, F])
        sbc = sb("sbc", [P, N])
        G = sb("G", [P, T, 4, FD], F16)
        adj_ring = sb("adj_ring", [P, RING, JG, CW], I32)
        rings = sb("rings", [P, T * F])
        h = rings[:, :].rearrange("p (t f) -> p t f", f=F)
        half = T * F // 2
        maskA = rings[:, 0:half].bitcast(BF16).rearrange("p (s q i) -> p s q i", s=RING, q=JG)
        maskB = rings[:, half:2 * half].bitcast(BF16).rearrange("p (s q i) -> p s q i", s=RING, q=JG)
        scratch = sb("scratch", [P, IB * FD + IB * F])
        comb = scratch[:, 0:IB * FD].rearrange("p (b f) -> p b f", f=FD)
        lone = scratch[:, IB * FD:].rearrange("p (b f) -> p b f", f=F)
        hn = [scratch[:, k * QUAD * F:(k + 1) * QUAD * F].rearrange("p (t f) -> p t f", f=F) for k in range(2)]
        hnT = [scratch[:, (2 + k) * QUAD * F:(3 + k) * QUAD * F] for k in range(2)]
        stats = scratch[:, 0:T * 6].rearrange("p (t s) -> p t s", s=6)
        moments = scratch[:, T * 6:T * 8].rearrange("p (t s) -> p t s", s=2)
        Wc = sb("Wc", [P, F])
        WTc = sb("WTc", [P, F])
        ac = sb("ac", [P, 2])
        rep = sb("rep", [P, F])
        Wsrc = sb("Wsrc", [P, F])
        Wa = sb("Wa", [P, 2])
        ident = sb("ident", [P, P])
        mean_h = sb("mean_h", [P, F])
        small = [sb(f"small{n}", [P, T]) for n in range(2)]
        rstd = sb("rstd", [P, T])
        shift = sb("shift", [P, T])
        sd = sb("sd", [P, T, 2])
        steep_d = sb("steep_d", [P, T])
        R = sb("R", [P, T])
        wA = sb("wA", [P, T])
        wB = sb("wB", [P, T])
        cA = sb("cA", [P, T], I32)
        icA = sb("icA", [P, T], I32)
        wAq = sb("wAq", [P, T])
        wBq = sb("wBq", [P, T])
        hsum = sb("hsum", [P, QUADS])
        col = sb("col", [P, 8])
        top_d, D, fro, fro_all, q0, hs = (col[:, n:n + 1] for n in range(6))
        q = sb("q", [P, 1], I32)
        no_nb = sb("no_nb", [P, IB])
        den_q = sb("den_q", [P, IB])
        inv = sb("inv", [P, IB])
        acc = ctx.enter_context(nc.psum_tensor("acc", [P, IB, 512], F32))

        w_landed = sem("w_landed")
        x_landed = sem("x_landed")
        adj_landed = [sem(f"adj_landed{k}") for k in range(RING)]
        stored = sem("stored")
        ident_made = sem("ident_made")
        dve_step = sem("dve_step")
        w_ready = sem("w_ready")
        wa_in_psum = sem("wa_in_psum")
        fro_ready = sem("fro_ready")
        fro_summed = sem("fro_summed")
        var_ready = sem("var_ready")
        sqrt_ready = sem("sqrt_ready")
        rstd_ready = sem("rstd_ready")
        hn_ready = sem("hn_ready")
        transposed = sem("transposed")
        hnT_ready = sem("hnT_ready")
        projected = sem("projected")
        quad_free = sem("quad_free")
        wa_ready = sem("wa_ready")
        stats_made = sem("stats_made")
        moments_made = sem("moments_made")
        top_ready = sem("top_ready")
        D_ready = sem("D_ready")
        exp_in = sem("exp_in")
        exp_ready = sem("exp_ready")
        hs_ready = sem("hs_ready")
        mean_in_psum = sem("mean_in_psum")
        scales_ready = sem("scales_ready")
        highA_ready = sem("highA_ready")
        highB_ready = sem("highB_ready")
        parts_ready = sem("parts_ready")
        relu_done = sem("relu_done")
        conv_done = sem("conv_done")
        a_made = sem("a_made")
        ab_ready = sem("ab_ready")
        ab_free = sem("ab_free")
        acc_ready = sem("acc_ready")
        bank_free = sem("bank_free")
        b_scaled = sem("b_scaled")
        comb_ready = sem("comb_ready")
        no_nb_ready = sem("no_nb_ready")
        den_ready = sem("den_ready")
        inv_ready = sem("inv_ready")
        o_ready = sem("o_ready")
        lone_ready = sem("lone_ready")
        lone_added = sem("lone_added")
        x_done = sem("x_done")

        def settle(eng, value):
            value = eng.snap(eng.to_reg(value))
            eng.wait_ge(x_landed, 16 * CHUNKS)
            return value

        block = ctx.enter_context(nc.Block())

        @block.sync
        def _(sp):
            for c in range(CHUNKS):
                sp.dma_start(X[:, c * IB:(c + 1) * IB, :], x_tiles[:, c * IB:(c + 1) * IB, :]).then_inc(x_landed, 16)

            def load_round(layer, r):
                for k in range(RING):
                    if layer is not None:
                        sp.wait_ge(conv_done, (layer * CHUNKS * ROUNDS + r - 1) * RING + k + 1)
                    sp.dma_start(adj_ring[:, k, :, :].rearrange("p q i -> p (q i)"),
                                 adj[bass.ds(r * RING + k, 1), :, :].rearrange("o p n -> (o p) n"))\
                      .then_inc(adj_landed[k], 16)

            def load_weights(layer):
                if layer is not None:
                    sp.wait_ge(parts_ready, layer * QUADS)
                l = 0 if layer is None else layer
                sp.dma_start(Wc[:, :], W[l, :, :]).then_inc(w_landed, 16)
                sp.dma_start(WTc[:, :], WT[l, :, :]).then_inc(w_landed, 16)
                sp.dma_start(ac[:, :], a[l, :, :]).then_inc(w_landed, 16)

            load_weights(None)
            load_round(None, 0)
            with sp.Fori(1, CHUNKS * ROUNDS) as r:
                load_round(0, r)
            for layer in range(1, LAYERS):
                load_weights(layer)
                with sp.Fori(0, CHUNKS * ROUNDS) as r:
                    load_round(layer, r)
            with sp.Fori(0, CHUNKS) as c:
                sp.wait_ge(x_done, c + ((LAYERS - 1) * CHUNKS + 2))
                sp.dma_start(out_tiles[:, bass.ds(c * IB, IB), :], X[:, bass.ds(c * IB, IB), :]).then_inc(stored, 16)
            sp.wait_ge(stored, 16 * CHUNKS)

        @block.gpsimd
        def _(pool):
            nc.gpsimd.memset(ident[:, :], 0.0).then_inc(ident_made, 1)
            pool.wait_ge(ident_made, 1)
            nc.gpsimd.affine_select(out=ident[:, :], in_=ident[:, :], compare_op=ALU.not_equal, fill=1.0,
                                    base=0, pattern=[[-1, P]], channel_multiplier=1).then_inc(ident_made, 1)
            pool.sem_inc(x_done, 1)
            with pool.Fori(0, LAYERS) as l:
                pool.wait_ge(fro_ready, settle(pool, l + 1))
                nc.gpsimd.partition_all_reduce(fro_all, fro, P, RADD).then_inc(fro_summed, 1)
                pool.wait_ge(top_ready, settle(pool, l + 1))
                nc.gpsimd.partition_all_reduce(D, top_d, P, RMAX).then_inc(D_ready, 1)
                pool.wait_ge(scales_ready, settle(pool, l + 1))
                with pool.Fori(0, QUADS) as n:
                    t0 = n * QUAD
                    nc.gpsimd.tensor_tensor(G[:, bass.ds(t0, QUAD), 2, 0:F], h[:, bass.ds(t0, QUAD), :],
                                            wBq[:, bass.ds(t0, QUAD)].unsqueeze(2).to_broadcast([P, QUAD, F]),
                                            ALU.mult).then_inc(highB_ready, 1)
                with pool.Fori(0, CHUNKS) as c:
                    n = l * CHUNKS + c
                    rows = X[:, bass.ds(c * IB, IB), :]
                    pool.wait_ge(inv_ready, n + 1)
                    nc.gpsimd.tensor_tensor(lone, no_nb[:, :].unsqueeze(2).to_broadcast([P, IB, F]),
                                            mean_h[:, :].unsqueeze(1).to_broadcast([P, IB, F]),
                                            ALU.mult).then_inc(lone_ready, 1)
                    pool.wait_ge(lone_ready, settle(pool, n + 1))
                    nc.gpsimd.tensor_tensor(rows, rows, lone, ALU.add).then_inc(lone_added, 1)
                    pool.wait_ge(lone_added, settle(pool, n + 1))
                    pool.wait_ge(o_ready, n + 1)
                    nc.gpsimd.tensor_tensor(rows, rows, comb[:, :, 0:F], ALU.add).then_inc(x_done, 1)

        @block.scalar
        def _(act):
            def prepare(l):
                act.wait_ge(w_ready, l + 1)
                nc.scalar.activation(rep_junk, Wc[:, :], ACT.Square, accum_out=fro).then_inc(fro_ready, 1)
                act.wait_ge(var_ready, l + 1)
                nc.scalar.activation(small[1][:, :], small[0][:, :], ACT.Sqrt)
                nc.scalar.activation(q0, q0, ACT.Sqrt).then_inc(sqrt_ready, 1)
                act.wait_ge(rstd_ready, settle(act, l + 1))
                with act.Fori(0, QUADS // 2) as m:
                    for k in range(2):
                        n = l * QUADS + m * 2 + k
                        t0 = (m * 2 + k) * QUAD
                        for i in range(QUAD):
                            ins = nc.scalar.activation(hn[k][:, i, :], X[:, bass.ds(t0 + i, 1), :].rearrange("p o f -> p (o f)"),
                                                       ACT.Relu, bias=shift[:, bass.ds(t0 + i, 1)],
                                                       scale=rstd[:, bass.ds(t0 + i, 1)])
                        ins.then_inc(hn_ready, 1)
                        act.wait_ge(transposed, settle(act, n + 1))
                        act.wait_ge(quad_free, n + 1)
                        nc.scalar.activation(hnT[k], acc[:, k, :], ACT.Copy,
                                             accum_out=hsum[:, bass.ds(m * 2 + k, 1)]).then_inc(hnT_ready, 1)
                act.wait_ge(exp_in, l + 1)
                nc.scalar.activation(wA[:, :], small[0][:, :], ACT.Exp)
                nc.scalar.activation(wB[:, :], small[0][:, :], ACT.Exp, scale=SLOPE)
                nc.scalar.activation(R[:, :], small[1][:, :], ACT.Exp).then_inc(exp_ready, 1)
                act.wait_ge(scales_ready, settle(act, l + 1))
                with act.Fori(0, QUADS) as m:
                    for i in range(QUAD):
                        t = m * QUAD + i
                        ins = nc.scalar.activation(G[:, bass.ds(t, 1), 0, 0:F].rearrange("p o f -> p (o f)"),
                                                   h[:, bass.ds(t, 1), :].rearrange("p o f -> p (o f)"),
                                                   ACT.Copy, scale=wAq[:, bass.ds(t, 1)])
                    ins.then_inc(highA_ready, 1)
                act.wait_ge(parts_ready, (l + 1) * QUADS)

            def group(l, c, r, k):
                n = ((l * CHUNKS + c) * ROUNDS + r) * RING + k
                act.wait_ge(ab_free, settle(act, n + 1))
                for j in range(JG):
                    ins = nc.scalar.activation(maskA[:, k, j, :], sbc[:, bass.ds(c * CW, CW)], ACT.Relu,
                                               bias=steep_d[:, bass.ds((r * RING + k) * JG + j, 1)])
                ins.then_inc(relu_done, 1)

            def evacuate(l, c):
                n = l * CHUNKS + c
                act.wait_ge(x_done, n + 1)
                for b in range(IB):
                    if b < IB - 1:
                        act.wait_ge(acc_ready, settle(act, n * (IB - 1) + b + 1))
                    else:
                        act.wait_ge(ab_free, settle(act, (n + 1) * GROUPS + RING))
                    nc.scalar.activation(comb[:, b, :], acc[:, b, FD:2 * FD], ACT.Copy,
                                         scale=R[:, bass.ds(c * IB + b, 1)]).then_inc(b_scaled, 1)

            def normalise(l, c):
                n = l * CHUNKS + c
                act.wait_ge(inv_ready, n + 1)
                for b in range(IB):
                    ins = nc.scalar.activation(comb[:, b, 0:F], comb[:, b, 0:F], ACT.Copy, scale=inv[:, b:b + 1])
                ins.then_inc(o_ready, 1)

            def chunk(l, c, first):
                for k in range(RING):
                    group(l, c, 0, k)
                    if k == 1 and not first:
                        evacuate(l, c - 1)
                if not first:
                    normalise(l, c - 1)
                with act.Fori(1, ROUNDS) as r:
                    for k in range(RING):
                        group(l, c, r, k)

            rep_junk = mean_h[:, :]
            with act.Fori(0, LAYERS) as l:
                prepare(l)
                chunk(l, 0, True)
                with act.Fori(1, CHUNKS) as c:
                    chunk(l, c, False)
                evacuate(l, CHUNKS - 1)
                normalise(l, CHUNKS - 1)

        @block.tensor
        def _(pe):
            def prepare(l):
                pe.wait_ge(w_ready, l + 1)
                nc.tensor.matmul(acc[:, 5, 0:2], WTc[:, :], ac[:, :], start=True, stop=True)
                nc.tensor.matmul(acc[:, 5, F:2 * F], WTc[:, :], rep[:, :], start=True, stop=True)\
                  .then_inc(wa_in_psum, 1)
                pe.wait_ge(wa_ready, settle(pe, l + 1))
                with pe.Fori(0, QUADS // 2) as m:
                    for k in range(2):
                        n = l * QUADS + m * 2 + k
                        pe.wait_ge(hn_ready, n + 1)
                        for i in range(QUAD):
                            ins = nc.tensor.transpose(acc[:, k, i * P:(i + 1) * P], hn[k][:, i, :], ident[:, :])
                        ins.then_inc(transposed, 1)
                        pe.wait_ge(hnT_ready, n + 1)
                        pe.wait_ge(quad_free, n + 1)
                        for i in range(QUAD):
                            nc.tensor.matmul(acc[:, 2 + k, i * F:(i + 1) * F], hnT[k][:, i * P:(i + 1) * P], Wc[:, :],
                                             start=True, stop=True)
                            nc.tensor.matmul(acc[:, 6 + k, 2 * i:2 * i + 2], hnT[k][:, i * P:(i + 1) * P],
                                             Wa[:, :], start=True, stop=True)
                        nc.tensor.matmul(acc[:, 4 + k, :], Wsrc[:, :], hnT[k], start=True, stop=True)\
                          .then_inc(projected, 1)
                pe.wait_ge(hs_ready, l + 1)
                nc.tensor.matmul(acc[:, 7, 0:F], rep[:, :], Wc[:, :], start=True, stop=True).then_inc(mean_in_psum, 1)
                pe.wait_ge(parts_ready, settle(pe, (l + 1) * QUADS))

            def group(l, c, r, k, first=False, last=False):
                n = ((l * CHUNKS + c) * ROUNDS + r) * RING + k
                pe.wait_ge(ab_ready, n + 1)
                for b in range(IB):
                    if first:
                        pe.wait_ge(bank_free, (l * CHUNKS + c) * IB + b + 1)
                    for j in range(JG):
                        t = (r * RING + k) * JG + j
                        for side, mask in enumerate((maskA, maskB)):
                            for part in range(2):
                                ins = nc.tensor.matmul(acc[:, b, side * FD:(side + 1) * FD], mask[:, k, j, b * P:(b + 1) * P],
                                                       G[:, bass.ds(t, 1), 2 * side + part, :].rearrange("p o f -> p (o f)"),
                                                       start=first and j == 0 and side == 0 and part == 0,
                                                       stop=last and j == JG - 1 and part == 1, skip_group_check=True)
                    if last and b < IB - 1:
                        ins.then_inc(acc_ready, 1)
                ins.then_inc(ab_free, 1)

            def chunk(l, c):
                for k in range(RING):
                    group(l, c, 0, k, first=k == 0)
                with pe.Fori(1, ROUNDS - 1) as r:
                    for k in range(RING):
                        group(l, c, r, k)
                for k in range(RING):
                    group(l, c, ROUNDS - 1, k, last=k == RING - 1)

            pe.wait_ge(ident_made, 2)
            pe.sem_inc(ab_free, RING)
            pe.sem_inc(bank_free, IB)
            with pe.Fori(0, LAYERS) as l:
                prepare(l)
                with pe.Fori(0, CHUNKS) as c:
                    chunk(l, c)

        @block.vector
        def _(dve):
            qf = q[:, :].bitcast(F32)
            s_col, d_col = sd[:, :, 0], sd[:, :, 1]

            def prepare(l):
                links = [0]

                def link(ins):
                    links[0] += 1
                    ins.then_inc(dve_step, 1)
                    dve.wait_ge(dve_step, l * DVE_STEPS + links[0])

                dve.wait_ge(x_done, l * CHUNKS + 1)
                dve.wait_ge(x_landed, 16 * CHUNKS)
                dve.wait_ge(w_landed, (l + 1) * 48)
                nc.vector.tensor_copy(rep[:, :], ac[:, 0:1].to_broadcast([P, F])).then_inc(w_ready, 1)
                with dve.Fori(0, T // 8) as m:
                    for i in range(8):
                        t = m * 8 + i
                        ins = nc.vector.bn_stats(stats[:, bass.ds(t, 1), :].rearrange("p o s -> p (o s)"),
                                                 X[:, bass.ds(t, 1), :].rearrange("p o f -> p (o f)"))
                    ins.then_inc(stats_made, 1)
                dve.wait_ge(stats_made, settle(dve, (l + 1) * (T // 8)))
                for t in range(T):
                    ins = nc.vector.bn_aggr(moments[:, t, :], stats[:, t, :])
                ins.then_inc(moments_made, 1)
                dve.wait_ge(moments_made, l + 1)
                nc.vector.tensor_scalar(small[0][:, :], moments[:, :, 1], LN_EPS, None, ALU.add)
                dve.wait_ge(fro_summed, l + 1)
                nc.vector.tensor_scalar(q0, fro_all, 1e-30, None, ALU.max).then_inc(var_ready, 1)
                dve.wait_ge(wa_in_psum, l + 1)
                nc.vector.tensor_copy(Wa[:, :], acc[:, 5, 0:2])
                nc.vector.tensor_copy(Wsrc[:, :], acc[:, 5, F:2 * F]).then_inc(wa_ready, 1)
                dve.wait_ge(sqrt_ready, l + 1)
                link(nc.vector.reciprocal(rstd[:, :], small[1][:, :]))
                link(nc.vector.tensor_tensor(small[1][:, :], rstd[:, :], rstd[:, :], ALU.mult))
                link(nc.vector.tensor_tensor(small[1][:, :], small[1][:, :], small[0][:, :], ALU.mult))
                link(nc.vector.tensor_scalar(small[1][:, :], small[1][:, :], -0.5, 1.5, ALU.mult, ALU.add))
                link(nc.vector.tensor_tensor(rstd[:, :], rstd[:, :], small[1][:, :], ALU.mult))
                nc.vector.scalar_tensor_tensor(shift[:, :], moments[:, :, 0], -1.0, rstd[:, :],
                                               ALU.mult, ALU.mult).then_inc(rstd_ready, 1)
                link(nc.vector.reciprocal(q0, q0))
                link(nc.vector.tensor_scalar(q0, q0, FP16_ROOM, None, ALU.mult))
                nc.vector.tensor_scalar(q[:, :], q0.bitcast(I32), EXPONENT_BITS, None, ALU.bitwise_and)
                with dve.Fori(0, QUADS // 2) as m:
                    for k in range(2):
                        t0 = (m * 2 + k) * QUAD
                        dve.wait_ge(projected, l * QUADS + m * 2 + k + 1)
                        nc.vector.tensor_copy(h[:, bass.ds(t0, QUAD), :].rearrange("p t f -> p (t f)"), acc[:, 2 + k, :])
                        nc.vector.tensor_copy(sd[:, bass.ds(t0, QUAD), :].rearrange("p t f -> p (t f)"),
                                              acc[:, 6 + k, 0:2 * QUAD])
                        nc.vector.tensor_scalar(sbc[:, bass.ds(t0 * P, QUAD * P)], acc[:, 4 + k, :], STEEP, None,
                                                ALU.mult).then_inc(quad_free, 1)
                dve.wait_ge(quad_free, (l + 1) * QUADS + 2)
                nc.vector.tensor_reduce(top_d, d_col, AX_X, ALU.max).then_inc(top_ready, 1)
                link(nc.vector.tensor_reduce(hs, hsum[:, :], AX_X, ALU.add))
                nc.vector.tensor_scalar(rep[:, :], hs.to_broadcast([P, F]), 1.0 / N, None, ALU.mult).then_inc(hs_ready, 1)
                nc.vector.tensor_scalar(steep_d[:, :], d_col, STEEP, None, ALU.mult)
                dve.wait_ge(D_ready, l + 1)
                nc.vector.tensor_scalar(small[0][:, :], d_col, D, None, ALU.subtract)
                link(nc.vector.tensor_scalar(small[1][:, :], s_col, D, SLOPE - 1.0, ALU.add, ALU.mult))
                nc.vector.tensor_scalar(small[1][:, :], small[1][:, :], 0.0, None, ALU.min).then_inc(exp_in, 1)
                dve.wait_ge(exp_ready, l + 1)
                link(nc.vector.tensor_scalar(cA[:, :], wA[:, :].bitcast(I32), EXPONENT_BITS, None, ALU.bitwise_and))
                link(nc.vector.tensor_scalar(cA[:, :], cA[:, :], LEAST_NORMAL_BITS, None, ALU.max))
                link(nc.vector.tensor_scalar(icA[:, :], cA[:, :], -1.0, ONE_SQUARED_BITS, ALU.mult, ALU.add))
                link(nc.vector.tensor_tensor(wA[:, :], wA[:, :], icA[:, :].bitcast(F32), ALU.mult))
                nc.vector.tensor_scalar(wAq[:, :], wA[:, :], qf, None, ALU.mult)
                nc.vector.tensor_scalar(wBq[:, :], wB[:, :], qf, None, ALU.mult).then_inc(scales_ready, 1)
                nc.vector.tensor_copy(G[:, :, 0, F], wA[:, :])
                link(nc.vector.tensor_copy(G[:, :, 2, F], wB[:, :]))
                nc.vector.tensor_tensor(G[:, :, 1, F], wA[:, :], G[:, :, 0, F], ALU.subtract)
                nc.vector.tensor_tensor(G[:, :, 3, F], wB[:, :], G[:, :, 2, F], ALU.subtract)
                dve.wait_ge(mean_in_psum, l + 1)
                nc.vector.tensor_copy(mean_h[:, :], acc[:, 7, 0:F])
                with dve.Fori(0, QUADS) as m:
                    dve.wait_ge(highA_ready, l * QUADS + m + 1)
                    dve.wait_ge(highB_ready, l * QUADS + m + 1)
                    for i in range(QUAD):
                        t = m * QUAD + i
                        for side, w in enumerate((wAq, wBq)):
                            high, low = (G[:, bass.ds(t, 1), 2 * side + part, 0:F].rearrange("p o f -> p (o f)")
                                         for part in range(2))
                            ins = nc.vector.scalar_tensor_tensor(low, h[:, bass.ds(t, 1), :].rearrange("p o f -> p (o f)"),
                                                                 w[:, bass.ds(t, 1)], high, ALU.mult, ALU.subtract)
                    ins.then_inc(parts_ready, 1)
                dve.wait_ge(parts_ready, settle(dve, (l + 1) * QUADS))
                assert links[0] == DVE_STEPS, links[0]

            def group(l, c, r, k):
                done = ((l * CHUNKS + c) * ROUNDS + r)
                n = done * RING + k
                dve.wait_ge(adj_landed[k], done * 16 + 16)
                dve.wait_ge(ab_free, n + 1)
                for j in range(JG):
                    ins = nc.vector.tensor_scalar(maskB[:, k, j, :], adj_ring[:, k, j, :], 0.0,
                                                  cA[:, bass.ds((r * RING + k) * JG + j, 1)].bitcast(F32),
                                                  ALU.is_gt, ALU.mult)
                ins.then_inc(conv_done, 1)
                dve.wait_ge(relu_done, n + 1)
                dve.wait_ge(conv_done, n + 1)
                nc.vector.tensor_tensor(maskA[:, k, :, :], maskA[:, k, :, :], maskB[:, k, :, :], ALU.min).then_inc(a_made, 1)
                dve.wait_ge(a_made, n + 1)
                nc.vector.tensor_tensor(maskB[:, k, :, :], maskA[:, k, :, :], maskB[:, k, :, :], ALU.is_lt)\
                  .then_inc(ab_ready, 1)

            def evacuate(l, c):
                n = l * CHUNKS + c
                for b in range(IB):
                    dve.wait_ge(b_scaled, n * IB + b + 1)
                    nc.vector.tensor_tensor(comb[:, b, :], comb[:, b, :], acc[:, b, 0:FD], ALU.add).then_inc(bank_free, 1)
                dve.wait_ge(bank_free, (n + 2) * IB)
                nc.vector.tensor_scalar(no_nb[:, :], comb[:, :, F], 0.0, None, ALU.is_equal).then_inc(no_nb_ready, 1)
                dve.wait_ge(no_nb_ready, n + 1)
                nc.vector.scalar_tensor_tensor(den_q[:, :], comb[:, :, F], qf, no_nb[:, :], ALU.mult, ALU.add)\
                  .then_inc(den_ready, 1)
                dve.wait_ge(den_ready, n + 1)
                nc.vector.reciprocal(inv[:, :], den_q[:, :]).then_inc(inv_ready, 1)

            def chunk(l, c, first):
                for k in range(RING):
                    group(l, c, 0, k)
                    if k == 1 and not first:
                        evacuate(l, c - 1)
                with dve.Fori(1, ROUNDS) as r:
                    for k in range(RING):
                        group(l, c, r, k)

            dve.sem_inc(quad_free, 2)
            with dve.Fori(0, LAYERS) as l:
                prepare(l)
                chunk(l, 0, True)
                with dve.Fori(1, CHUNKS) as c:
                    chunk(l, c, False)
                evacuate(l, CHUNKS - 1)

    return nc


def kernel(x, adj, L0_gnn_W, L0_gnn_a, L1_gnn_W, L1_gnn_a):
    import numpy as np
    import concourse.bacc as bacc
    from concourse.bass_utils import run_bass_kernel_spmd

    x, adj = np.asarray(x), np.asarray(adj)
    N, F = x.shape
    CW = IB * P
    W = np.stack([np.asarray(L0_gnn_W), np.asarray(L1_gnn_W)])
    a = np.stack([np.asarray(L0_gnn_a), np.asarray(L1_gnn_a)])
    blocks = adj.reshape(N // CW, CW, N // (JG * P), JG, P).transpose(0, 2, 4, 3, 1)
    arrays = {
        "x": np.ascontiguousarray(x),
        "adj": np.ascontiguousarray(blocks).reshape(-1, P, JG * CW),
        "W": np.ascontiguousarray(W),
        "WT": np.ascontiguousarray(W.transpose(0, 2, 1)),
        "a": np.ascontiguousarray(a.reshape(2, 2, F).transpose(0, 2, 1)),
    }
    nc = bacc.Bacc("TRN2", target_bir_lowering=False, num_devices=1)
    args = [nc.dram_tensor(n, v.shape, mybir.dt.from_np(v.dtype), kind="ExternalInput").ap() for n, v in arrays.items()]
    out = nc.dram_tensor("out", x.shape, F32, kind="ExternalOutput").ap()
    gat2_kernel(nc, *args, out)
    r = run_bass_kernel_spmd(nc, [arrays], core_ids=[0])
    return r.results[0]["out"]
```

```python
from contextlib import ExitStack

import concourse.bass as bass
from concourse import mybir

P = 128
ALU = mybir.AluOpType
ACT = mybir.ActivationFunctionType
F32 = mybir.dt.float32
F16 = mybir.dt.float16
BF16 = mybir.dt.bfloat16
I32 = mybir.dt.int32
AX_X = mybir.AxisListType.X
RMAX = bass.bass_isa.ReduceOp.max
RADD = bass.bass_isa.ReduceOp.add

SLOPE = 0.2
LN_EPS = 1e-5
STEEP = 2.0 ** 100
EXPONENT_BITS = 0x7F800000
ONE_SQUARED_BITS = float(0x7F000000)
LEAST_NORMAL_BITS = float(0x00800000)
FP16_ROOM = 2500.0

RING = 4
JG = 2
IB = 8
SIGNED = (0, 1, 2)
QUAD = 4


def gat2_kernel(nc, x, adj, W, WT, a, out):
    N, F = x.shape
    LAYERS = W.shape[0]
    T = N // P
    CHUNKS = T // IB
    CW = IB * P
    GROUPS = T // JG
    ROUNDS = GROUPS // RING
    QUADS = T // QUAD
    FD = F + 1
    OCTETS = [o for k in range(RING) for o in (k, RING + k)]
    DVE_STEPS = 14
    assert F == P and T == 2 * RING * IB and GROUPS % RING == 0 and ROUNDS >= 3 and QUADS % 2 == 0

    x_tiles = x.rearrange("(t p) f -> p t f", p=P)
    out_tiles = out.rearrange("(t p) f -> p t f", p=P)

    with ExitStack() as ctx:
        def sb(name, shape, dt=F32):
            return ctx.enter_context(nc.sbuf_tensor(name, shape, dt))

        def sem(name):
            return ctx.enter_context(nc.semaphore(name))

        X = sb("X", [P, T, F])
        sbc = sb("sbc", [P, N])
        G = sb("G", [P, T, 4, FD], F16)
        adj_ring = sb("adj_ring", [P, RING, JG, CW], I32)
        rings = sb("rings", [P, T * F])
        h = rings[:, :].rearrange("p (t f) -> p t f", f=F)
        half = T * F // 2
        maskA = rings[:, 0:half].bitcast(BF16).rearrange("p (s q i) -> p s q i", s=RING, q=JG)
        maskB = rings[:, half:2 * half].bitcast(BF16).rearrange("p (s q i) -> p s q i", s=RING, q=JG)
        scratch = sb("scratch", [P, IB * FD + IB * F])
        comb = scratch[:, 0:IB * FD].rearrange("p (b f) -> p b f", f=FD)
        lone = scratch[:, IB * FD:].rearrange("p (b f) -> p b f", f=F)
        hn = [scratch[:, k * QUAD * F:(k + 1) * QUAD * F].rearrange("p (t f) -> p t f", f=F) for k in range(2)]
        hnT = [scratch[:, (2 + k) * QUAD * F:(3 + k) * QUAD * F] for k in range(2)]
        stats = sb("stats", [P, IB, 6])
        mv = sb("mv", [P, IB, 2])
        moments = sb("moments", [P, T, 2])
        Wc = sb("Wc", [P, F])
        WTc = sb("WTc", [P, F])
        ac = sb("ac", [P, 2])
        rep = sb("rep", [P, F])
        Wsrc = WTc
        Wa = sb("Wa", [P, 2])
        ident = sb("ident", [P, P])
        mean_h = sb("mean_h", [P, F])
        small = [sb(f"small{n}", [P, T]) for n in range(2)]
        rstd = sb("rstd", [P, T])
        shift = sb("shift", [P, T])
        sd = sb("sd", [P, T, 2])
        steep_d = sb("steep_d", [P, T])
        R = sb("R", [P, T])
        wA = sb("wA", [P, T])
        wB = sb("wB", [P, T])
        cA = sb("cA", [P, T + JG], I32)
        icA = sb("icA", [P, T], I32)
        wAq = sb("wAq", [P, T])
        wBq = sb("wBq", [P, T])
        hsum = sb("hsum", [P, QUADS])
        col = sb("col", [P, 8])
        top_d, D, fro, fro_all, q0, hs = (col[:, n:n + 1] for n in range(6))
        q = sb("q", [P, 1], I32)
        no_nb = sb("no_nb", [P, IB])
        den_q = sb("den_q", [P, IB])
        inv = sb("inv", [P, IB])
        acc = ctx.enter_context(nc.psum_tensor("acc", [P, IB, 512], F32))

        w_landed = sem("w_landed")
        x_landed = [sem(f"x_landed{c}") for c in range(CHUNKS)]
        adj_landed = [sem(f"adj_landed{k}") for k in range(RING)]
        stored = sem("stored")
        ident_made = sem("ident_made")
        dve_step = sem("dve_step")
        w_ready = sem("w_ready")
        wa_in_psum = sem("wa_in_psum")
        fro_ready = sem("fro_ready")
        fro_summed = sem("fro_summed")
        var_ready = sem("var_ready")
        sqrt_ready = sem("sqrt_ready")
        rstd_ready = sem("rstd_ready")
        hn_ready = sem("hn_ready")
        transposed = sem("transposed")
        hnT_ready = sem("hnT_ready")
        projected = sem("projected")
        quad_free = sem("quad_free")
        wa_ready = sem("wa_ready")
        stats_made = sem("stats_made")
        moments_made = sem("moments_made")
        moments_copied = sem("moments_copied")
        top_ready = sem("top_ready")
        D_ready = sem("D_ready")
        exp_in = sem("exp_in")
        row_exp_in = sem("row_exp_in")
        exp_ready = sem("exp_ready")
        hs_ready = sem("hs_ready")
        mean_in_psum = sem("mean_in_psum")
        scales_ready = sem("scales_ready")
        highA_ready = sem("highA_ready")
        highB_ready = sem("highB_ready")
        parts_ready = sem("parts_ready")
        relu_done = sem("relu_done")
        sign_done = sem("sign_done")
        conv_done = sem("conv_done")
        a_made = sem("a_made")
        ab_ready = sem("ab_ready")
        ab_free = sem("ab_free")
        acc_ready = sem("acc_ready")
        bank_free = sem("bank_free")
        b_scaled = sem("b_scaled")
        comb_ready = sem("comb_ready")
        no_nb_ready = sem("no_nb_ready")
        den_ready = sem("den_ready")
        inv_ready = sem("inv_ready")
        o_ready = sem("o_ready")
        lone_ready = sem("lone_ready")
        lone_added = sem("lone_added")
        x_done = sem("x_done")

        def settle(eng, value):
            value = eng.snap(eng.to_reg(value))
            eng.wait_ge(x_landed[0], 16)
            return value

        block = ctx.enter_context(nc.Block())

        @block.sync
        def _(sp):
            def load_round(layer, r):
                for k in range(RING):
                    if layer is not None:
                        sp.wait_ge(conv_done, (layer * CHUNKS * ROUNDS + r - 1) * RING + k + 1)
                    sp.dma_start(adj_ring[:, k, :, :].rearrange("p q i -> p (q i)"),
                                 adj[bass.ds(r * RING + k, 1), :, :].rearrange("o p n -> (o p) n"))\
                      .then_inc(adj_landed[k], 16)

            def load_weights(layer):
                if layer is not None:
                    sp.wait_ge(parts_ready, layer * CHUNKS)
                l = 0 if layer is None else layer
                sp.dma_start(Wc[:, :], W[l, :, :]).then_inc(w_landed, 16)
                sp.dma_start(WTc[:, :], WT[l, :, :]).then_inc(w_landed, 16)
                sp.dma_start(ac[:, :], a[l, :, :]).then_inc(w_landed, 16)

            load_weights(None)
            for c in range(CHUNKS):
                sp.dma_start(X[:, c * IB:(c + 1) * IB, :], x_tiles[:, c * IB:(c + 1) * IB, :]).then_inc(x_landed[c], 16)
            load_round(None, 0)
            with sp.Fori(1, CHUNKS * ROUNDS) as r:
                load_round(0, r)
            for layer in range(1, LAYERS):
                load_weights(layer)
                with sp.Fori(0, CHUNKS * ROUNDS) as r:
                    load_round(layer, r)
            with sp.Fori(0, CHUNKS) as c:
                sp.wait_ge(x_done, c + ((LAYERS - 1) * CHUNKS + 2))
                sp.dma_start(out_tiles[:, bass.ds(c * IB, IB), :], X[:, bass.ds(c * IB, IB), :]).then_inc(stored, 16)
            sp.wait_ge(stored, 16 * CHUNKS)

        @block.gpsimd
        def _(pool):
            nc.gpsimd.memset(ident[:, :], 0.0).then_inc(ident_made, 1)
            pool.wait_ge(ident_made, 1)
            nc.gpsimd.affine_select(out=ident[:, :], in_=ident[:, :], compare_op=ALU.not_equal, fill=1.0,
                                    base=0, pattern=[[-1, P]], channel_multiplier=1).then_inc(ident_made, 1)
            pool.sem_inc(x_done, 1)
            with pool.Fori(0, LAYERS) as l:
                pool.wait_ge(fro_ready, settle(pool, l + 1))
                nc.gpsimd.partition_all_reduce(fro_all, fro, P, RADD).then_inc(fro_summed, 1)
                pool.wait_ge(top_ready, settle(pool, l + 1))
                nc.gpsimd.partition_all_reduce(D, top_d, P, RMAX).then_inc(D_ready, 1)
                pool.wait_ge(scales_ready, settle(pool, l + 1))
                for o in OCTETS:
                    t0 = o * IB
                    nc.gpsimd.tensor_tensor(G[:, t0:t0 + IB, 2, 0:F], h[:, t0:t0 + IB, :],
                                            wBq[:, t0:t0 + IB].unsqueeze(2).to_broadcast([P, IB, F]),
                                            ALU.mult).then_inc(highB_ready, 1)
                with pool.Fori(0, CHUNKS) as c:
                    n = l * CHUNKS + c
                    rows = X[:, bass.ds(c * IB, IB), :]
                    pool.wait_ge(inv_ready, n + 1)
                    nc.gpsimd.tensor_tensor(comb[:, :, 0:F], comb[:, :, 0:F], inv[:, :].unsqueeze(2).to_broadcast([P, IB, F]),
                                            ALU.mult).then_inc(o_ready, 1)
                    nc.gpsimd.tensor_tensor(lone, no_nb[:, :].unsqueeze(2).to_broadcast([P, IB, F]),
                                            mean_h[:, :].unsqueeze(1).to_broadcast([P, IB, F]),
                                            ALU.mult).then_inc(lone_ready, 1)
                    pool.wait_ge(lone_ready, settle(pool, n + 1))
                    nc.gpsimd.tensor_tensor(rows, rows, lone, ALU.add).then_inc(lone_added, 1)
                    pool.wait_ge(lone_added, settle(pool, n + 1))
                    pool.wait_ge(o_ready, n + 1)
                    nc.gpsimd.tensor_tensor(rows, rows, comb[:, :, 0:F], ALU.add).then_inc(x_done, 1)

        @block.scalar
        def _(act):
            def prepare(l):
                act.wait_ge(w_ready, l + 1)
                nc.scalar.activation(rep_junk, Wc[:, :], ACT.Square, accum_out=fro).then_inc(fro_ready, 1)
                act.wait_ge(var_ready, l + 1)
                nc.scalar.activation(small[1][:, :], small[0][:, :], ACT.Sqrt)
                nc.scalar.activation(q0, q0, ACT.Sqrt).then_inc(sqrt_ready, 1)
                act.wait_ge(rstd_ready, settle(act, l + 1))

                def normalised(m, k):
                    t0 = (m * 2 + k) * QUAD
                    for i in range(QUAD):
                        ins = nc.scalar.activation(hn[k][:, i, :], X[:, bass.ds(t0 + i, 1), :].rearrange("p o f -> p (o f)"),
                                                   ACT.Relu, bias=shift[:, bass.ds(t0 + i, 1)],
                                                   scale=rstd[:, bass.ds(t0 + i, 1)])
                    ins.then_inc(hn_ready, 1)

                def from_psum(m, k):
                    n = l * QUADS + m * 2 + k
                    act.wait_ge(transposed, settle(act, n + 1))
                    act.wait_ge(quad_free, n + 1)
                    nc.scalar.activation(hnT[k], acc[:, k, :], ACT.Copy,
                                         accum_out=hsum[:, bass.ds(m * 2 + k, 1)]).then_inc(hnT_ready, 1)

                normalised(0, 0)
                with act.Fori(0, QUADS // 2 - 1) as m:
                    normalised(m, 1)
                    from_psum(m, 0)
                    normalised(m + 1, 0)
                    from_psum(m, 1)
                normalised(QUADS // 2 - 1, 1)
                from_psum(QUADS // 2 - 1, 0)
                from_psum(QUADS // 2 - 1, 1)
                act.wait_ge(exp_in, l + 1)
                nc.scalar.activation(wA[:, :], small[0][:, :], ACT.Exp)
                nc.scalar.activation(wB[:, :], small[0][:, :], ACT.Exp, scale=SLOPE).then_inc(exp_ready, 1)
                act.wait_ge(row_exp_in, l + 1)
                nc.scalar.activation(R[:, :], small[1][:, :], ACT.Exp)
                act.wait_ge(scales_ready, l + 1)
                for o in OCTETS[0:2]:
                    high(o)

            def high(o):
                for t in range(o * IB, (o + 1) * IB):
                    ins = nc.scalar.activation(G[:, t, 0, 0:F], h[:, t, :], ACT.Copy, scale=wAq[:, t:t + 1])
                ins.then_inc(highA_ready, 1)

            def group(l, c, r, k, fresh=False):
                n = ((l * CHUNKS + c) * ROUNDS + r) * RING + k
                if fresh:
                    act.wait_ge(parts_ready, l * CHUNKS + 2 * k + 2)
                act.wait_ge(ab_free, settle(act, n + 1))
                if k in SIGNED:
                    act.wait_ge(adj_landed[k], (n - k) * (16 // RING) + 16)
                    nc.scalar.activation(maskB[:, k, JG - 1, :], adj_ring[:, k, JG - 1, :], ACT.Sign).then_inc(sign_done, 1)
                for j in range(JG):
                    ins = nc.scalar.activation(maskA[:, k, j, :], sbc[:, bass.ds(c * CW, CW)], ACT.Relu,
                                               bias=steep_d[:, bass.ds((r * RING + k) * JG + j, 1)])
                ins.then_inc(relu_done, 1)

            def evacuate(l, c):
                n = l * CHUNKS + c
                act.wait_ge(x_done, n + 1)
                for b in range(IB):
                    if b < IB - 1:
                        act.wait_ge(acc_ready, settle(act, n * (IB - 1) + b + 1))
                    else:
                        act.wait_ge(ab_free, settle(act, (n + 1) * GROUPS + RING))
                    nc.scalar.activation(comb[:, b, :], acc[:, b, FD:2 * FD], ACT.Copy,
                                         scale=R[:, bass.ds(c * IB + b, 1)]).then_inc(b_scaled, 1)

            def chunk(l, c, first):
                for k in range(RING):
                    group(l, c, 0, k, fresh=first)
                    if first and 2 * k + 2 < CHUNKS:
                        high(OCTETS[2 * k + 2])
                        high(OCTETS[2 * k + 3])
                    if k == RING - 2 and not first:
                        evacuate(l, c - 1)
                with act.Fori(1, ROUNDS) as r:
                    for k in range(RING):
                        group(l, c, r, k)

            rep_junk = mean_h[:, :]
            with act.Fori(0, LAYERS) as l:
                prepare(l)
                chunk(l, 0, True)
                with act.Fori(1, CHUNKS) as c:
                    chunk(l, c, False)
                evacuate(l, CHUNKS - 1)

        @block.tensor
        def _(pe):
            def prepare(l):
                pe.wait_ge(w_ready, l + 1)
                nc.tensor.matmul(acc[:, 5, 0:2], WTc[:, :], ac[:, :], start=True, stop=True)
                nc.tensor.matmul(acc[:, 5, F:2 * F], WTc[:, :], rep[:, :], start=True, stop=True)\
                  .then_inc(wa_in_psum, 1)
                pe.wait_ge(wa_ready, settle(pe, l + 1))

                def transposes(m, k):
                    pe.wait_ge(hn_ready, l * QUADS + m * 2 + k + 1)
                    for i in range(QUAD):
                        ins = nc.tensor.transpose(acc[:, k, i * P:(i + 1) * P], hn[k][:, i, :], ident[:, :])
                    ins.then_inc(transposed, 1)

                def projections(m, k):
                    n = l * QUADS + m * 2 + k
                    pe.wait_ge(hnT_ready, n + 1)
                    pe.wait_ge(quad_free, n + 1)
                    for i in range(QUAD):
                        nc.tensor.matmul(acc[:, 2 + k, i * F:(i + 1) * F], hnT[k][:, i * P:(i + 1) * P], Wc[:, :],
                                         start=True, stop=True)
                        nc.tensor.matmul(acc[:, 6 + k, 2 * i:2 * i + 2], hnT[k][:, i * P:(i + 1) * P],
                                         Wa[:, :], start=True, stop=True)
                    nc.tensor.matmul(acc[:, 4 + k, :], Wsrc[:, :], hnT[k], start=True, stop=True)\
                      .then_inc(projected, 1)

                transposes(0, 0)
                with pe.Fori(0, QUADS // 2 - 1) as m:
                    transposes(m, 1)
                    projections(m, 0)
                    transposes(m + 1, 0)
                    projections(m, 1)
                transposes(QUADS // 2 - 1, 1)
                projections(QUADS // 2 - 1, 0)
                projections(QUADS // 2 - 1, 1)
                pe.wait_ge(hs_ready, l + 1)
                nc.tensor.matmul(acc[:, 7, 0:F], rep[:, :], Wc[:, :], start=True, stop=True).then_inc(mean_in_psum, 1)

            def group(l, c, r, k, first=False, last=False):
                n = ((l * CHUNKS + c) * ROUNDS + r) * RING + k
                pe.wait_ge(ab_ready, n + 1)
                for b in range(IB):
                    if first:
                        pe.wait_ge(bank_free, (l * CHUNKS + c) * IB + b + 1)
                    for j in range(JG):
                        t = (r * RING + k) * JG + j
                        for side, mask in enumerate((maskA, maskB)):
                            for part in range(2):
                                ins = nc.tensor.matmul(acc[:, b, side * FD:(side + 1) * FD], mask[:, k, j, b * P:(b + 1) * P],
                                                       G[:, bass.ds(t, 1), 2 * side + part, :].rearrange("p o f -> p (o f)"),
                                                       start=first and j == 0 and side == 0 and part == 0,
                                                       stop=last and j == JG - 1 and part == 1, skip_group_check=True)
                    if last and b < IB - 1:
                        ins.then_inc(acc_ready, 1)
                ins.then_inc(ab_free, 1)

            def chunk(l, c):
                for k in range(RING):
                    group(l, c, 0, k, first=k == 0)
                with pe.Fori(1, ROUNDS - 1) as r:
                    for k in range(RING):
                        group(l, c, r, k)
                for k in range(RING):
                    group(l, c, ROUNDS - 1, k, last=k == RING - 1)

            pe.wait_ge(ident_made, 2)
            pe.sem_inc(ab_free, RING)
            pe.sem_inc(bank_free, IB)
            with pe.Fori(0, LAYERS) as l:
                prepare(l)
                with pe.Fori(0, CHUNKS) as c:
                    chunk(l, c)

        @block.vector
        def _(dve):
            qf = q[:, :].bitcast(F32)
            s_col, d_col = sd[:, :, 0], sd[:, :, 1]

            def row_moments(n, t0):
                for b in range(IB):
                    ins = nc.vector.bn_stats(stats[:, b, :], X[:, bass.ds(t0 + b, 1), :].rearrange("p o f -> p (o f)"))
                ins.then_inc(stats_made, 1)
                dve.wait_ge(stats_made, n + 1 if isinstance(n, int) else settle(dve, n + 1))
                for b in range(IB):
                    ins = nc.vector.bn_aggr(mv[:, b, :], stats[:, b, :])
                ins.then_inc(moments_made, 1)
                dve.wait_ge(moments_made, n + 1)
                nc.vector.tensor_copy(moments[:, bass.ds(t0, IB), :], mv[:, :, :]).then_inc(moments_copied, 1)

            def prepare(l):
                links = [0]

                def link(ins):
                    links[0] += 1
                    ins.then_inc(dve_step, 1)
                    dve.wait_ge(dve_step, l * DVE_STEPS + links[0])

                dve.wait_ge(x_done, l * CHUNKS + 1)
                dve.wait_ge(w_landed, (l + 1) * 48)
                nc.vector.tensor_copy(rep[:, :], ac[:, 0:1].to_broadcast([P, F])).then_inc(w_ready, 1)
                dve.wait_ge(x_landed[CHUNKS - 1], 16)
                row_moments(l * CHUNKS + CHUNKS - 1, (CHUNKS - 1) * IB)
                dve.wait_ge(moments_copied, (l + 1) * CHUNKS)
                nc.vector.tensor_scalar(small[0][:, :], moments[:, :, 1], LN_EPS, None, ALU.add)
                dve.wait_ge(fro_summed, l + 1)
                nc.vector.tensor_scalar(q0, fro_all, 1e-30, None, ALU.max).then_inc(var_ready, 1)
                dve.wait_ge(wa_in_psum, l + 1)
                nc.vector.tensor_copy(Wa[:, :], acc[:, 5, 0:2])
                nc.vector.tensor_copy(Wsrc[:, :], acc[:, 5, F:2 * F]).then_inc(wa_ready, 1)
                dve.wait_ge(sqrt_ready, l + 1)
                link(nc.vector.reciprocal(rstd[:, :], small[1][:, :]))
                link(nc.vector.tensor_tensor(small[1][:, :], rstd[:, :], rstd[:, :], ALU.mult))
                link(nc.vector.tensor_tensor(small[1][:, :], small[1][:, :], small[0][:, :], ALU.mult))
                link(nc.vector.tensor_scalar(small[1][:, :], small[1][:, :], -0.5, 1.5, ALU.mult, ALU.add))
                link(nc.vector.tensor_tensor(rstd[:, :], rstd[:, :], small[1][:, :], ALU.mult))
                nc.vector.scalar_tensor_tensor(shift[:, :], moments[:, :, 0], -1.0, rstd[:, :],
                                               ALU.mult, ALU.mult).then_inc(rstd_ready, 1)
                link(nc.vector.reciprocal(q0, q0))
                link(nc.vector.tensor_scalar(q0, q0, FP16_ROOM, None, ALU.mult))
                nc.vector.tensor_scalar(q[:, :], q0.bitcast(I32), EXPONENT_BITS, None, ALU.bitwise_and)
                with dve.Fori(0, QUADS // 2) as m:
                    for k in range(2):
                        t0 = (m * 2 + k) * QUAD
                        dve.wait_ge(projected, l * QUADS + m * 2 + k + 1)
                        nc.vector.tensor_copy(h[:, bass.ds(t0, QUAD), :].rearrange("p t f -> p (t f)"), acc[:, 2 + k, :])
                        nc.vector.tensor_copy(sd[:, bass.ds(t0, QUAD), :].rearrange("p t f -> p (t f)"),
                                              acc[:, 6 + k, 0:2 * QUAD])
                        nc.vector.tensor_scalar(sbc[:, bass.ds(t0 * P, QUAD * P)], acc[:, 4 + k, :], STEEP, None,
                                                ALU.mult).then_inc(quad_free, 1)
                dve.wait_ge(quad_free, (l + 1) * QUADS + 2)
                nc.vector.tensor_reduce(top_d, d_col, AX_X, ALU.max).then_inc(top_ready, 1)
                link(nc.vector.tensor_reduce(hs, hsum[:, :], AX_X, ALU.add))
                nc.vector.tensor_scalar(rep[:, :], hs.to_broadcast([P, F]), 1.0 / N, None, ALU.mult).then_inc(hs_ready, 1)
                nc.vector.tensor_scalar(steep_d[:, :], d_col, STEEP, None, ALU.mult)
                dve.wait_ge(D_ready, l + 1)
                nc.vector.tensor_scalar(small[0][:, :], d_col, D, None, ALU.subtract).then_inc(exp_in, 1)
                link(nc.vector.tensor_scalar(small[1][:, :], s_col, D, SLOPE - 1.0, ALU.add, ALU.mult))
                nc.vector.tensor_scalar(small[1][:, :], small[1][:, :], 0.0, None, ALU.min).then_inc(row_exp_in, 1)
                dve.wait_ge(exp_ready, l + 1)
                link(nc.vector.tensor_scalar(cA[:, 0:T], wA[:, :].bitcast(I32), EXPONENT_BITS, None, ALU.bitwise_and))
                link(nc.vector.tensor_scalar(cA[:, 0:T], cA[:, 0:T], LEAST_NORMAL_BITS, None, ALU.max))
                nc.vector.tensor_copy(cA[:, T:T + JG], cA[:, 0:JG])
                link(nc.vector.tensor_scalar(icA[:, :], cA[:, 0:T], -1.0, ONE_SQUARED_BITS, ALU.mult, ALU.add))
                link(nc.vector.tensor_tensor(wA[:, :], wA[:, :], icA[:, :].bitcast(F32), ALU.mult))
                nc.vector.tensor_scalar(wAq[:, :], wA[:, :], qf, None, ALU.mult)
                nc.vector.tensor_scalar(wBq[:, :], wB[:, :], qf, None, ALU.mult).then_inc(scales_ready, 1)
                nc.vector.tensor_copy(G[:, :, 0, F], wA[:, :])
                link(nc.vector.tensor_copy(G[:, :, 2, F], wB[:, :]))
                nc.vector.tensor_tensor(G[:, :, 1, F], wA[:, :], G[:, :, 0, F], ALU.subtract)
                nc.vector.tensor_tensor(G[:, :, 3, F], wB[:, :], G[:, :, 2, F], ALU.subtract)
                dve.wait_ge(mean_in_psum, l + 1)
                nc.vector.tensor_copy(mean_h[:, :], acc[:, 7, 0:F])
                assert links[0] == DVE_STEPS, links[0]

            def low(l, o):
                for high_ready in (highA_ready, highB_ready):
                    dve.wait_ge(high_ready, l * CHUNKS + OCTETS.index(o) + 1)
                for t in range(o * IB, (o + 1) * IB):
                    for side, w in enumerate((wAq, wBq)):
                        ins = nc.vector.scalar_tensor_tensor(G[:, t, 2 * side + 1, 0:F], h[:, t, :], w[:, t:t + 1],
                                                             G[:, t, 2 * side, 0:F], ALU.mult, ALU.subtract)
                ins.then_inc(parts_ready, 1)

            def edges(l, c, r, k, fresh=False):
                if fresh and k < RING:
                    dve.wait_ge(parts_ready, l * CHUNKS + 2 * k + 2)
                if k == RING:
                    r, k = r + 1, 0
                done = (l * CHUNKS + c) * ROUNDS + r
                dve.wait_ge(adj_landed[k], done * 16 + 16)
                dve.wait_ge(ab_free, done * RING + k + 1)
                tile0 = (r * RING + k) * JG
                for j in range(JG - (k in SIGNED)):
                    ins = nc.vector.tensor_scalar(maskB[:, k, j, :], adj_ring[:, k, j, :], 0.0,
                                                  cA[:, bass.ds(tile0 + j, 1)].bitcast(F32), ALU.is_gt, ALU.mult)
                if k in SIGNED:
                    dve.wait_ge(sign_done, done * len(SIGNED) + SIGNED.index(k) + 1)
                    ins = nc.vector.tensor_scalar(maskB[:, k, JG - 1, :], maskB[:, k, JG - 1, :], 0.0,
                                                  cA[:, bass.ds(tile0 + JG - 1, 1)].bitcast(F32), ALU.max, ALU.mult)
                ins.then_inc(conv_done, 1)

            def group(l, c, r, k, more=True):
                n = ((l * CHUNKS + c) * ROUNDS + r) * RING + k
                dve.wait_ge(relu_done, n + 1)
                dve.wait_ge(conv_done, n + 1)
                nc.vector.tensor_tensor(maskA[:, k, :, :], maskA[:, k, :, :], maskB[:, k, :, :], ALU.min).then_inc(a_made, 1)
                if more:
                    edges(l, c, r, k + 1)
                dve.wait_ge(a_made, n + 1)
                nc.vector.tensor_tensor(maskB[:, k, :, :], maskA[:, k, :, :], maskB[:, k, :, :], ALU.is_lt)\
                  .then_inc(ab_ready, 1)

            def evacuate(l, c):
                n = l * CHUNKS + c
                for b in range(IB):
                    dve.wait_ge(b_scaled, n * IB + b + 1)
                    nc.vector.tensor_tensor(comb[:, b, :], comb[:, b, :], acc[:, b, 0:FD], ALU.add).then_inc(bank_free, 1)

            def denominators(l, c):
                n = l * CHUNKS + c
                dve.wait_ge(bank_free, (n + 2) * IB)
                nc.vector.tensor_scalar(no_nb[:, :], comb[:, :, F], 0.0, None, ALU.is_equal).then_inc(no_nb_ready, 1)
                dve.wait_ge(no_nb_ready, n + 1)
                nc.vector.scalar_tensor_tensor(den_q[:, :], comb[:, :, F], qf, no_nb[:, :], ALU.mult, ALU.add)\
                  .then_inc(den_ready, 1)
                dve.wait_ge(den_ready, n + 1)
                nc.vector.reciprocal(inv[:, :], den_q[:, :]).then_inc(inv_ready, 1)

            def chunk(l, c, first=False, last=False):
                for k in range(RING):
                    group(l, c, 0, k, more=not first)
                    if first:
                        if k < RING - 1:
                            low(l, OCTETS[2 * k + 2])
                            low(l, OCTETS[2 * k + 3])
                        edges(l, c, 0, k + 1, fresh=True)
                    elif k == 1:
                        evacuate(l, c - 1)
                if not first:
                    denominators(l, c - 1)
                with dve.Fori(1, ROUNDS // 2) as r:
                    for k in range(RING):
                        group(l, c, r, k)
                if not first:
                    dve.wait_ge(x_done, l * CHUNKS + c + 1)
                    row_moments((l + 1) * CHUNKS + c - 1, (c - 1) * IB)
                with dve.Fori(ROUNDS // 2, ROUNDS - last) as r:
                    for k in range(RING):
                        group(l, c, r, k)
                if last:
                    for k in range(RING):
                        group(l, c, ROUNDS - 1, k, more=k < RING - 1)

            dve.sem_inc(quad_free, 2)
            for c in range(CHUNKS - 1):
                dve.wait_ge(x_landed[c], 16)
                row_moments(c, c * IB)
            with dve.Fori(0, LAYERS) as l:
                prepare(l)
                for o in OCTETS[0:2]:
                    low(l, o)
                edges(l, 0, 0, 0, fresh=True)
                chunk(l, 0, first=True)
                with dve.Fori(1, CHUNKS - 1) as c:
                    chunk(l, c)
                chunk(l, CHUNKS - 1, last=True)
                evacuate(l, CHUNKS - 1)
                denominators(l, CHUNKS - 1)

    return nc


def kernel(x, adj, L0_gnn_W, L0_gnn_a, L1_gnn_W, L1_gnn_a):
    import numpy as np
    import concourse.bacc as bacc
    from concourse.bass_utils import run_bass_kernel_spmd

    x, adj = np.asarray(x), np.asarray(adj)
    N, F = x.shape
    CW = IB * P
    W = np.stack([np.asarray(L0_gnn_W), np.asarray(L1_gnn_W)])
    a = np.stack([np.asarray(L0_gnn_a), np.asarray(L1_gnn_a)])
    blocks = adj.reshape(N // CW, CW, N // (JG * P), JG, P).transpose(0, 2, 4, 3, 1)
    arrays = {
        "x": np.ascontiguousarray(x),
        "adj": np.ascontiguousarray(blocks).reshape(-1, P, JG * CW),
        "W": np.ascontiguousarray(W),
        "WT": np.ascontiguousarray(W.transpose(0, 2, 1)),
        "a": np.ascontiguousarray(a.reshape(2, 2, F).transpose(0, 2, 1)),
    }
    nc = bacc.Bacc("TRN2", target_bir_lowering=False, num_devices=1)
    args = [nc.dram_tensor(n, v.shape, mybir.dt.from_np(v.dtype), kind="ExternalInput").ap() for n, v in arrays.items()]
    out = nc.dram_tensor("out", x.shape, F32, kind="ExternalOutput").ap()
    gat2_kernel(nc, *args, out)
    r = run_bass_kernel_spmd(nc, [arrays], core_ids=[0])
    return r.results[0]["out"]
```

```python
from contextlib import ExitStack

import concourse.bass as bass
from concourse import mybir

P = 128
ALU = mybir.AluOpType
ACT = mybir.ActivationFunctionType
F32 = mybir.dt.float32
F16 = mybir.dt.float16
BF16 = mybir.dt.bfloat16
I32 = mybir.dt.int32
AX_X = mybir.AxisListType.X
RMAX = bass.bass_isa.ReduceOp.max
RADD = bass.bass_isa.ReduceOp.add

SLOPE = 0.2
LN_EPS = 1e-5
STEEP = 2.0 ** 100
RSQRT_BITS = float(0x5F3759DF)
EXPONENT_BITS = 0x7F800000
ONE_SQUARED_BITS = float(0x7F000000)
LEAST_NORMAL_BITS = float(0x00800000)
FP16_ROOM = 2500.0

RING = 4
JG = 2
IB = 8
EARLY = 1
SIGNED = (0, 1, 2, 3)
QUAD = 4


def gat2_kernel(nc, x, adj, W, WT, a, out):
    N, F = x.shape
    LAYERS = W.shape[0]
    T = N // P
    CHUNKS = T // IB
    CW = IB * P
    GROUPS = T // JG
    ROUNDS = GROUPS // RING
    QUADS = T // QUAD
    FD = F + 1
    OCTETS = T // IB
    LAST = OCTETS - 1
    POOL_STEPS = 2 * OCTETS
    assert all(4 * FD * IB * (o + 1) <= T * (4 * FD - 2 * F) + 2 * F * IB * o for o in range(LAST))
    ROOT_STEPS = 11
    BEFORE_LAST = (CHUNKS - 1) * IB
    DVE_STEPS = 8
    assert F == P and OCTETS == ROUNDS == CHUNKS and GROUPS % RING == 0 and RING == 4
    assert ROUNDS % 2 == 0 and ROUNDS >= 4 and QUADS % 2 == 0

    x_tiles = x.rearrange("(t p) f -> p t f", p=P)
    out_tiles = out.rearrange("(t p) f -> p t f", p=P)

    with ExitStack() as ctx:
        def sb(name, shape, dt=F32):
            return ctx.enter_context(nc.sbuf_tensor(name, shape, dt))

        def sem(name):
            return ctx.enter_context(nc.semaphore(name))

        X = sb("X", [P, T, F])
        sbc = sb("sbc", [P, N])
        Gh = sb("Gh", [P, T * 4 * FD], F16)
        G = Gh[:, :].rearrange("p (t a f) -> p t a f", a=4, f=FD)
        h = Gh[:, T * (4 * FD - 2 * F):].bitcast(F32).rearrange("p (t f) -> p t f", f=F)
        adj_ring = sb("adj_ring", [P, RING, JG, CW], I32)
        maskA = sb("maskA", [P, RING, JG, CW], BF16)
        maskB = sb("maskB", [P, RING, JG, CW], BF16)
        scratch = sb("scratch", [P, IB * FD + IB * F])
        comb = scratch[:, 0:IB * FD].rearrange("p (b f) -> p b f", f=FD)
        hn_space = Gh[:, 0:4 * QUAD * F * 2].bitcast(F32)
        hn = [hn_space[:, k * QUAD * F:(k + 1) * QUAD * F].rearrange("p (t f) -> p t f", f=F) for k in range(2)]
        hnT = [hn_space[:, (2 + k) * QUAD * F:(3 + k) * QUAD * F] for k in range(2)]
        stats = sb("stats", [P, IB, 6])
        mv = sb("mv", [P, IB, 2])
        moments = sb("moments", [P, T, 2])
        lone = scratch[:, IB * FD:].rearrange("p (b f) -> p b f", f=F)
        split = comb
        last_h = scratch[:, IB * FD:].rearrange("p (b f) -> p b f", f=F)
        WWa = sb("WWa", [P, F + 2])
        Wc, Wa = WWa[:, 0:F], WWa[:, F:F + 2]
        WTc = sb("WTc", [P, F])
        ac = sb("ac", [P, 2])
        rep = sb("rep", [P, F])
        Wsrc = WTc
        ident = sb("ident", [P, P])
        mean_h = sb("mean_h", [P, F])
        small = [sb(f"small{n}", [P, T + 1 - n]) for n in range(2)]
        spread = sb("spread", [P, T + 1])
        rstd = sb("rstd", [P, T + 1])
        newton = small[0]
        shift = sb("shift", [P, T])
        sd = sb("sd", [P, T, 2])
        steep_d = sb("steep_d", [P, T])
        R = sb("R", [P, T])
        wA = sb("wA", [P, T])
        wB = sb("wB", [P, T])
        cA = sb("cA", [P, T + JG], I32)
        icA = small[0][:, 0:T].bitcast(I32)
        wAq = sb("wAq", [P, T])
        wBq = sb("wBq", [P, T])
        hsum = sb("hsum", [P, QUADS])
        col = sb("col", [P, 8])
        top_d, D, fro, fro_all, q0, hs = (col[:, n:n + 1] for n in range(6))
        q = sb("q", [P, 1], I32)
        no_nb = sb("no_nb", [P, IB])
        den_q = sb("den_q", [P, IB])
        inv = sb("inv", [P, IB])
        acc = ctx.enter_context(nc.psum_tensor("acc", [P, IB, 512], F32))

        w_landed = sem("w_landed")
        x_landed = [sem(f"x_landed{c}") for c in range(CHUNKS)]
        adj_landed = [sem(f"adj_landed{k}") for k in range(RING)]
        stored = sem("stored")
        ident_made = sem("ident_made")
        dve_step = sem("dve_step")
        w_ready = sem("w_ready")
        wa_in_psum = sem("wa_in_psum")
        fro_ready = sem("fro_ready")
        fro_summed = sem("fro_summed")
        w_squared = sem("w_squared")
        root_step = sem("root_step")
        rstd_ready = sem("rstd_ready")
        hn_ready = sem("hn_ready")
        transposed = sem("transposed")
        hnT_ready = sem("hnT_ready")
        projected = sem("projected")
        quad_free = sem("quad_free")
        wa_ready = sem("wa_ready")
        stats_made = sem("stats_made")
        moments_made = sem("moments_made")
        moments_copied = sem("moments_copied")
        top_ready = sem("top_ready")
        D_ready = sem("D_ready")
        exp_in = sem("exp_in")
        row_exp_in = sem("row_exp_in")
        exp_ready = sem("exp_ready")
        hs_ready = sem("hs_ready")
        mean_in_psum = sem("mean_in_psum")
        scales_ready = sem("scales_ready")
        last_h_ready = sem("last_h_ready")
        highs_ready = sem("highs_ready")
        columns_ready = sem("columns_ready")
        highA_ready = sem("highA_ready")
        steep_ready = sem("steep_ready")
        partsA_ready = sem("partsA_ready")
        partsB_ready = sem("partsB_ready")
        relu_done = sem("relu_done")
        sign_done = sem("sign_done")
        conv_done = sem("conv_done")
        a_made = sem("a_made")
        ab_ready = sem("ab_ready")
        ab_free = sem("ab_free")
        acc_ready = sem("acc_ready")
        bank_free = sem("bank_free")
        b_scaled = sem("b_scaled")
        pool_step = sem("pool_step")
        o_ready = sem("o_ready")
        lone_ready = sem("lone_ready")
        lone_added = sem("lone_added")
        hi_added = sem("hi_added")
        no_nb_ready = sem("no_nb_ready")
        den_ready = sem("den_ready")
        inv_ready = sem("inv_ready")
        attention_added = sem("attention_added")
        x_done = sem("x_done")

        def settle(eng, value):
            value = eng.snap(eng.to_reg(value))
            eng.wait_ge(x_landed[0], 16)
            return value

        block = ctx.enter_context(nc.Block())

        @block.sync
        def _(sp):
            def load_round(layer, r):
                for k in range(RING):
                    if layer is not None:
                        sp.wait_ge(conv_done, (layer * CHUNKS * ROUNDS + r - 1) * RING + k + 1)
                    sp.dma_start(adj_ring[:, k, :, :].rearrange("p q i -> p (q i)"),
                                 adj[bass.ds(r * RING + k, 1), :, :].rearrange("o p n -> (o p) n"))\
                      .then_inc(adj_landed[k], 16)

            def load_weights(layer):
                if layer is not None:
                    sp.wait_ge(partsA_ready, layer * OCTETS + 1)
                l = 0 if layer is None else layer
                sp.dma_start(Wc[:, :], W[l, :, :]).then_inc(w_landed, 16)
                sp.dma_start(WTc[:, :], WT[l, :, :]).then_inc(w_landed, 16)
                sp.dma_start(ac[:, :], a[l, :, :]).then_inc(w_landed, 16)

            for c in range(CHUNKS):
                sp.dma_start(X[:, c * IB:(c + 1) * IB, :], x_tiles[:, c * IB:(c + 1) * IB, :]).then_inc(x_landed[c], 16)
                if c == 0:
                    load_weights(None)
            load_round(None, 0)
            with sp.Fori(1, CHUNKS * ROUNDS) as r:
                load_round(0, r)
            for layer in range(1, LAYERS):
                load_weights(layer)
                with sp.Fori(0, CHUNKS * ROUNDS) as r:
                    load_round(layer, r)
            with sp.Fori(0, CHUNKS) as c:
                sp.wait_ge(x_done, c + ((LAYERS - 1) * CHUNKS + 2))
                sp.dma_start(out_tiles[:, bass.ds(c * IB, IB), :], X[:, bass.ds(c * IB, IB), :]).then_inc(stored, 16)
            sp.wait_ge(stored, 16 * CHUNKS)

        @block.gpsimd
        def _(pool):
            nc.gpsimd.memset(ident[:, :], 0.0).then_inc(ident_made, 1)
            pool.wait_ge(ident_made, 1)
            nc.gpsimd.affine_select(out=ident[:, :], in_=ident[:, :], compare_op=ALU.not_equal, fill=1.0,
                                    base=0, pattern=[[-1, P]], channel_multiplier=1).then_inc(ident_made, 1)
            pool.sem_inc(partsB_ready, 1)
            with pool.Fori(0, LAYERS) as l:
                pool.wait_ge(w_landed, settle(pool, (l + 1) * 48))
                nc.gpsimd.tensor_copy(rep[:, :], ac[:, 0:1].to_broadcast([P, F])).then_inc(w_ready, 1)
                pool.wait_ge(fro_ready, settle(pool, l + 1))
                nc.gpsimd.partition_all_reduce(fro_all, fro, P, RADD).then_inc(fro_summed, 1)
                pool.wait_ge(top_ready, settle(pool, l + 1))
                nc.gpsimd.partition_all_reduce(D, top_d, P, RMAX).then_inc(D_ready, 1)
                pool.wait_ge(scales_ready, settle(pool, l + 1))

                def link(ins, n):
                    ins.then_inc(pool_step, 1)
                    pool.wait_ge(pool_step, settle(pool, l * POOL_STEPS + n + 1))

                def side_B(o, src):
                    tiles = bass.ds(o * IB, IB)
                    w = wBq[:, tiles].unsqueeze(2).to_broadcast([P, IB, F])
                    pool.wait_ge(partsB_ready, settle(pool, l * OCTETS + o + 1))
                    nc.gpsimd.tensor_copy(split[:, :, F], wB[:, tiles])
                    link(nc.gpsimd.tensor_tensor(split[:, :, 0:F], src, w, ALU.mult), 2 * o)
                    pool.wait_ge(partsA_ready, settle(pool, l * OCTETS + o + 1))
                    nc.gpsimd.tensor_copy(G[:, tiles, 2, F], wB[:, tiles])
                    link(nc.gpsimd.tensor_tensor(G[:, tiles, 2, 0:F], src, w, ALU.mult), 2 * o + 1)
                    nc.gpsimd.tensor_tensor(G[:, tiles, 3, :], split, G[:, tiles, 2, :], ALU.subtract).then_inc(partsB_ready, 1)

                with pool.Fori(0, LAST) as o:
                    side_B(o, h[:, bass.ds(o * IB, IB), :])
                pool.wait_ge(partsB_ready, settle(pool, l * OCTETS + LAST + 1))
                nc.gpsimd.tensor_copy(last_h, h[:, LAST * IB:, :]).then_inc(last_h_ready, 1)
                pool.wait_ge(last_h_ready, settle(pool, l + 1))
                side_B(LAST, last_h)
                pool.wait_ge(partsA_ready, settle(pool, (l + 1) * OCTETS + 1))
                pool.wait_ge(partsB_ready, settle(pool, (l + 1) * OCTETS + 1))
                with pool.Fori(0, CHUNKS - 1) as c:
                    n = l * (CHUNKS - 1) + c
                    rows = X[:, bass.ds(c * IB, IB), :]
                    pool.wait_ge(inv_ready, l * CHUNKS + c + 1)
                    nc.gpsimd.tensor_tensor(comb[:, :, 0:F], comb[:, :, 0:F], inv[:, :].unsqueeze(2).to_broadcast([P, IB, F]),
                                            ALU.mult).then_inc(o_ready, 1)
                    nc.gpsimd.tensor_tensor(lone, no_nb[:, :].unsqueeze(2).to_broadcast([P, IB, F]),
                                            mean_h[:, :].unsqueeze(1).to_broadcast([P, IB, F]),
                                            ALU.mult).then_inc(lone_ready, 1)
                    pool.wait_ge(lone_ready, settle(pool, n + 1))
                    nc.gpsimd.tensor_tensor(rows, rows, lone, ALU.add).then_inc(lone_added, 1)
                    pool.wait_ge(lone_added, settle(pool, n + 1))
                    pool.wait_ge(o_ready, n + 1)
                    nc.gpsimd.tensor_tensor(rows, rows, comb[:, :, 0:F], ALU.add).then_inc(x_done, 1)

        @block.scalar
        def _(act):
            def prepare(l):
                act.wait_ge(rstd_ready, settle(act, l * 2 + 1))

                def normalised(m, k):
                    t0 = (m * 2 + k) * QUAD
                    for i in range(QUAD):
                        ins = nc.scalar.activation(hn[k][:, i, :], X[:, bass.ds(t0 + i, 1), :].rearrange("p o f -> p (o f)"),
                                                   ACT.Relu, bias=shift[:, bass.ds(t0 + i, 1)],
                                                   scale=rstd[:, bass.ds(t0 + i, 1)])
                    ins.then_inc(hn_ready, 1)

                def from_psum(m, k):
                    n = l * QUADS + m * 2 + k
                    act.wait_ge(transposed, settle(act, n + 1))
                    act.wait_ge(quad_free, n + 1)
                    nc.scalar.activation(hnT[k], acc[:, k, :], ACT.Copy,
                                         accum_out=hsum[:, bass.ds(m * 2 + k, 1)]).then_inc(hnT_ready, 1)

                normalised(0, 0)
                act.wait_ge(wa_in_psum, l + 1)
                nc.scalar.activation(Wa[:, :], acc[:, 5, 0:2], ACT.Copy)
                nc.scalar.activation(Wsrc[:, :], acc[:, 5, F:2 * F], ACT.Copy).then_inc(wa_ready, 1)
                with act.Fori(0, QUADS // 2 - 2) as m:
                    normalised(m, 1)
                    from_psum(m, 0)
                    normalised(m + 1, 0)
                    from_psum(m, 1)
                m = QUADS // 2 - 2
                normalised(m, 1)
                from_psum(m, 0)
                act.wait_ge(rstd_ready, settle(act, l * 2 + 2))
                normalised(m + 1, 0)
                from_psum(m, 1)
                normalised(m + 1, 1)
                from_psum(m + 1, 0)
                from_psum(m + 1, 1)
                act.wait_ge(exp_in, l + 1)
                nc.scalar.activation(wA[:, :], small[0][:, 0:T], ACT.Exp)
                nc.scalar.activation(wB[:, :], small[0][:, 0:T], ACT.Exp, scale=SLOPE).then_inc(exp_ready, 1)
                act.wait_ge(row_exp_in, l + 1)
                nc.scalar.activation(R[:, :], small[1][:, :], ACT.Exp)
                act.wait_ge(steep_ready, l + 1)
                group(l, 0, 0, 0)
                act.wait_ge(scales_ready, l + 1)
                for t in range(IB):
                    ins = nc.scalar.activation(G[:, t, 0, 0:F], h[:, t, :], ACT.Copy, scale=wAq[:, t:t + 1])
                ins.then_inc(highA_ready, 1)
                group(l, 0, 0, 1)

            def highs(l, o, half, last=False):
                act.wait_ge(partsA_ready, settle(act, l * OCTETS + o + 1))
                act.wait_ge(partsB_ready, settle(act, l * OCTETS + o + 1))
                if last:
                    act.wait_ge(last_h_ready, settle(act, l + 1))
                for i in range(half * IB // 2, (half + 1) * IB // 2):
                    t = o * IB + i
                    src = last_h[:, i, :] if last else h[:, bass.ds(t, 1), :].rearrange("p o f -> p (o f)")
                    ins = nc.scalar.activation(G[:, bass.ds(t, 1), 0, 0:F].rearrange("p o f -> p (o f)"), src,
                                               ACT.Copy, scale=wAq[:, bass.ds(t, 1)])
                ins.then_inc(highs_ready, 1)

            def group(l, c, r, k):
                n = ((l * CHUNKS + c) * ROUNDS + r) * RING + k
                act.wait_ge(ab_free, settle(act, n + 1))
                if k in SIGNED:
                    act.wait_ge(adj_landed[k], (n - k) * (16 // RING) + 16)
                    nc.scalar.activation(maskB[:, k, JG - 1, :], adj_ring[:, k, JG - 1, :], ACT.Sign).then_inc(sign_done, 1)
                for j in range(JG):
                    ins = nc.scalar.activation(maskA[:, k, j, :], sbc[:, bass.ds(c * CW, CW)], ACT.Relu,
                                               bias=steep_d[:, bass.ds((r * RING + k) * JG + j, 1)])
                ins.then_inc(relu_done, 1)

            def evacuate(l, c):
                n = l * CHUNKS + c
                act.wait_ge(x_done, n + 1)
                for b in range(IB):
                    if b < IB - 1:
                        act.wait_ge(acc_ready, settle(act, n * (IB - 1) + b + 1))
                    else:
                        act.wait_ge(ab_free, settle(act, (n + 1) * GROUPS + RING))
                    nc.scalar.activation(comb[:, b, :], acc[:, b, 2 * FD:3 * FD], ACT.Copy,
                                         scale=R[:, bass.ds(c * IB + b, 1)]).then_inc(b_scaled, 1)

            def first_chunk(l):
                def round_(r, k0=0, last=False):
                    for k in range(k0, RING):
                        if k >= 2:
                            highs(l, r + 1, k - 2, last)
                        group(l, 0, r, k)

                round_(0, 2)
                with act.Fori(1, ROUNDS - 2) as r:
                    round_(r)
                round_(ROUNDS - 2, last=True)
                for k in range(RING):
                    group(l, 0, ROUNDS - 1, k)

            def chunk(l, c):
                for k in range(RING):
                    group(l, c, 0, k)
                    if k == RING - 2:
                        evacuate(l, c - 1)
                with act.Fori(1, ROUNDS) as r:
                    for k in range(RING):
                        group(l, c, r, k)

            with act.Fori(0, LAYERS) as l:
                prepare(l)
                first_chunk(l)
                with act.Fori(1, CHUNKS) as c:
                    chunk(l, c)
                evacuate(l, CHUNKS - 1)

        @block.tensor
        def _(pe):
            def prepare(l):
                def transposes(m, k):
                    pe.wait_ge(hn_ready, l * QUADS + m * 2 + k + 1)
                    for i in range(QUAD):
                        ins = nc.tensor.transpose(acc[:, k, i * P:(i + 1) * P], hn[k][:, i, :], ident[:, :])
                    ins.then_inc(transposed, 1)

                def projections(m, k):
                    n = l * QUADS + m * 2 + k
                    pe.wait_ge(hnT_ready, n + 1)
                    pe.wait_ge(quad_free, n + 1)
                    for i in range(QUAD):
                        bank, at = (2 + k, i * (F + 2)) if i < QUAD - 1 else (6 + k, 0)
                        nc.tensor.matmul(acc[:, bank, at:at + F + 2], hnT[k][:, i * P:(i + 1) * P], WWa[:, :],
                                         start=True, stop=True)
                    nc.tensor.matmul(acc[:, 4 + k, :], Wsrc[:, :], hnT[k], start=True, stop=True)\
                      .then_inc(projected, 1)

                pe.wait_ge(bank_free, (l * CHUNKS + 1) * IB)
                pe.wait_ge(w_ready, l + 1)
                nc.tensor.matmul(acc[:, 5, 0:2], WTc[:, :], ac[:, :], start=True, stop=True)
                nc.tensor.matmul(acc[:, 5, F:2 * F], WTc[:, :], rep[:, :], start=True, stop=True)\
                  .then_inc(wa_in_psum, 1)
                transposes(0, 0)
                pe.wait_ge(wa_ready, settle(pe, l + 1))
                with pe.Fori(0, QUADS // 2 - 1) as m:
                    transposes(m, 1)
                    projections(m, 0)
                    transposes(m + 1, 0)
                    projections(m, 1)
                transposes(QUADS // 2 - 1, 1)
                projections(QUADS // 2 - 1, 0)
                projections(QUADS // 2 - 1, 1)
                pe.wait_ge(hs_ready, l + 1)
                nc.tensor.matmul(acc[:, 7, 0:F], rep[:, :], Wc[:, :], start=True, stop=True).then_inc(mean_in_psum, 1)

            def group(l, c, r, k, first=False, last=False):
                n = ((l * CHUNKS + c) * ROUNDS + r) * RING + k
                pe.wait_ge(ab_ready, n + 1)
                if k == 0:
                    pe.wait_ge(partsA_ready, l * OCTETS + r + 2)
                    pe.wait_ge(partsB_ready, l * OCTETS + r + 2)
                for b in range(IB):
                    if first:
                        pe.wait_ge(bank_free, (l * CHUNKS + c) * IB + b + 1)
                    for j in range(JG):
                        t = (r * RING + k) * JG + j
                        parts = G[:, bass.ds(t, 1), :, :].rearrange("p o a f -> p (o a f)")
                        for mask, to, part, count in ((maskA, 0, 0, 2), (maskB, 2, 2, 1), (maskB, 2, 3, 1)):
                            ins = nc.tensor.matmul(acc[:, b, to * FD:(to + count) * FD], mask[:, k, j, b * P:(b + 1) * P],
                                                   parts[:, part * FD:(part + count) * FD],
                                                   start=first and j == 0 and part == 0,
                                                   stop=last and j == JG - 1 and part != 2, skip_group_check=True)
                    if last and b < IB - 1:
                        ins.then_inc(acc_ready, 1)
                ins.then_inc(ab_free, 1)

            def chunk(l, c):
                for k in range(RING):
                    group(l, c, 0, k, first=k == 0)
                with pe.Fori(0, (ROUNDS - 2) // 2) as two:
                    for r in (two * 2 + 1, two * 2 + 2):
                        for k in range(RING):
                            group(l, c, r, k)
                for k in range(RING):
                    group(l, c, ROUNDS - 1, k, last=k == RING - 1)

            pe.wait_ge(ident_made, 2)
            pe.sem_inc(ab_free, RING)
            pe.sem_inc(bank_free, IB)
            with pe.Fori(0, LAYERS) as l:
                prepare(l)
                with pe.Fori(0, CHUNKS) as c:
                    chunk(l, c)

        @block.vector
        def _(dve):
            qf = q[:, :].bitcast(F32)
            s_col, d_col = sd[:, :, 0], sd[:, :, 1]

            def row_moments(n, t0):
                for b in range(IB):
                    ins = nc.vector.bn_stats(stats[:, b, :], X[:, bass.ds(t0 + b, 1), :].rearrange("p o f -> p (o f)"))
                ins.then_inc(stats_made, 1)
                dve.wait_ge(stats_made, n + 1 if isinstance(n, int) else settle(dve, n + 1))
                for b in range(IB):
                    ins = nc.vector.bn_aggr(mv[:, b, :], stats[:, b, :])
                ins.then_inc(moments_made, 1)
                dve.wait_ge(moments_made, n + 1)
                nc.vector.tensor_copy(moments[:, bass.ds(t0, IB), :], mv[:, :, :]).then_inc(moments_copied, 1)

            def roots(n, chunks, t0, t1, more=0):
                steps = [0]
                v, y, u = spread[:, t0:t1 + more], rstd[:, t0:t1 + more], newton[:, t0:t1 + more]

                def link(ins):
                    steps[0] += 1
                    ins.then_inc(root_step, 1)
                    dve.wait_ge(root_step, n * ROOT_STEPS + steps[0])

                dve.wait_ge(moments_copied, chunks)
                link(nc.vector.tensor_scalar(spread[:, t0:t1], moments[:, t0:t1, 1], LN_EPS, None, ALU.add))
                link(nc.vector.tensor_scalar(y.bitcast(I32), v.bitcast(I32), -0.5, RSQRT_BITS, ALU.mult, ALU.add))
                for _ in range(3):
                    link(nc.vector.scalar_tensor_tensor(u, y, -0.5, v, ALU.mult, ALU.mult))
                    link(nc.vector.tensor_tensor(u, u, y, ALU.mult))
                    link(nc.vector.scalar_tensor_tensor(y, u, 1.5, y, ALU.add, ALU.mult))
                assert steps[0] == ROOT_STEPS, steps[0]
                nc.vector.scalar_tensor_tensor(shift[:, t0:t1], moments[:, t0:t1, 0], -1.0, rstd[:, t0:t1],
                                               ALU.mult, ALU.mult).then_inc(rstd_ready, 1)

            def quads(l, m0, m1):
                with dve.Fori(m0, m1) as m:
                    for k in range(2):
                        t0 = (m * 2 + k) * QUAD
                        dve.wait_ge(projected, l * QUADS + m * 2 + k + 1)
                        for t1, count, bank in ((t0, QUAD - 1, 2 + k), (t0 + QUAD - 1, 1, 6 + k)):
                            got = acc[:, bank, 0:count * (F + 2)].rearrange("p (t f) -> p t f", f=F + 2)
                            nc.vector.tensor_copy(h[:, bass.ds(t1, count), :], got[:, :, 0:F])
                            nc.vector.tensor_copy(sd[:, bass.ds(t1, count), :], got[:, :, F:F + 2])
                        nc.vector.tensor_scalar(sbc[:, bass.ds(t0 * P, QUAD * P)], acc[:, 4 + k, :], STEEP, None,
                                                ALU.mult).then_inc(quad_free, 1)

            def prepare(l):
                links = [0]

                def link(ins):
                    links[0] += 1
                    ins.then_inc(dve_step, 1)
                    dve.wait_ge(dve_step, l * DVE_STEPS + links[0])

                dve.wait_ge(w_landed, (l + 1) * 48)
                dve.wait_ge(x_done, l * CHUNKS + 1)
                nc.vector.tensor_tensor(mean_h[:, :], Wc[:, :], Wc[:, :], ALU.mult).then_inc(w_squared, 1)
                dve.wait_ge(w_squared, l + 1)
                nc.vector.tensor_reduce(fro, mean_h[:, :], AX_X, ALU.add).then_inc(fro_ready, 1)
                quads(l, 0, EARLY)
                dve.wait_ge(x_landed[CHUNKS - 1], 16)
                row_moments(l * CHUNKS + CHUNKS - 1, BEFORE_LAST)
                quads(l, EARLY, EARLY + 1)
                dve.wait_ge(fro_summed, l + 1)
                nc.vector.tensor_scalar(spread[:, T:T + 1], fro_all, 1e-30, None, ALU.max)
                roots(l * 2 + 1, (l + 1) * CHUNKS, BEFORE_LAST, T, 1)
                link(nc.vector.tensor_scalar(q0, rstd[:, T:T + 1], FP16_ROOM, None, ALU.mult))
                nc.vector.tensor_scalar(q[:, :], q0.bitcast(I32), EXPONENT_BITS, None, ALU.bitwise_and)
                quads(l, EARLY + 1, QUADS // 2)
                dve.wait_ge(quad_free, (l + 1) * QUADS + 2)
                nc.vector.tensor_reduce(top_d, d_col, AX_X, ALU.max).then_inc(top_ready, 1)
                nc.vector.tensor_scalar(steep_d[:, :], d_col, STEEP, None, ALU.mult).then_inc(steep_ready, 1)
                link(nc.vector.tensor_reduce(hs, hsum[:, :], AX_X, ALU.add))
                nc.vector.tensor_scalar(rep[:, :], hs.to_broadcast([P, F]), 1.0 / N, None, ALU.mult).then_inc(hs_ready, 1)
                dve.wait_ge(D_ready, l + 1)
                nc.vector.tensor_scalar(small[0][:, 0:T], d_col, D, None, ALU.subtract).then_inc(exp_in, 1)
                link(nc.vector.tensor_scalar(small[1][:, :], s_col, D, SLOPE - 1.0, ALU.add, ALU.mult))
                nc.vector.tensor_scalar(small[1][:, :], small[1][:, :], 0.0, None, ALU.min).then_inc(row_exp_in, 1)
                dve.wait_ge(exp_ready, l + 1)
                link(nc.vector.tensor_scalar(cA[:, 0:T], wA[:, :].bitcast(I32), EXPONENT_BITS, None, ALU.bitwise_and))
                link(nc.vector.tensor_scalar(cA[:, 0:T], cA[:, 0:T], LEAST_NORMAL_BITS, None, ALU.max))
                nc.vector.tensor_copy(cA[:, T:T + JG], cA[:, 0:JG])
                link(nc.vector.tensor_scalar(icA, cA[:, 0:T], -1.0, ONE_SQUARED_BITS, ALU.mult, ALU.add))
                link(nc.vector.tensor_tensor(wA[:, :], wA[:, :], icA.bitcast(F32), ALU.mult))
                nc.vector.tensor_scalar(wAq[:, :], wA[:, :], qf, None, ALU.mult)
                nc.vector.tensor_scalar(wBq[:, :], wB[:, :], qf, None, ALU.mult).then_inc(scales_ready, 1)
                link(nc.vector.tensor_copy(G[:, 0:IB, 0, F], wA[:, 0:IB]))
                nc.vector.tensor_tensor(G[:, 0:IB, 1, F], wA[:, 0:IB], G[:, 0:IB, 0, F], ALU.subtract)
                dve.wait_ge(mean_in_psum, l + 1)
                nc.vector.tensor_copy(mean_h[:, :], acc[:, 7, 0:F])
                assert links[0] == DVE_STEPS, links[0]

            def lows(l, t0, count, src):
                for i in range(count):
                    ins = nc.vector.scalar_tensor_tensor(flat(G[:, bass.ds(t0 + i, 1), 1, 0:F]), src(i), wAq[:, bass.ds(t0 + i, 1)],
                                                         flat(G[:, bass.ds(t0 + i, 1), 0, 0:F]), ALU.mult, ALU.subtract)
                return ins

            def flat(rows):
                return rows.rearrange("p o f -> p (o f)")

            def first_lows(l):
                dve.wait_ge(highA_ready, l + 1)
                lows(l, 0, IB, lambda i: h[:, i, :]).then_inc(partsA_ready, 1)

            def low(l, o, half, last=False):
                n = l * LAST + o
                t0 = o * IB + half * IB // 2
                tiles = bass.ds(o * IB, IB)
                dve.wait_ge(highs_ready, (n - 1) * 2 + half + 1)
                if half == 0:
                    nc.vector.tensor_copy(G[:, tiles, 0, F], wA[:, tiles]).then_inc(columns_ready, 1)
                else:
                    dve.wait_ge(columns_ready, n)
                    nc.vector.tensor_tensor(G[:, tiles, 1, F], wA[:, tiles], G[:, tiles, 0, F], ALU.subtract)
                ins = lows(l, t0, IB // 2, lambda i: last_h[:, half * IB // 2 + i, :] if last else flat(h[:, bass.ds(t0 + i, 1), :]))
                if half:
                    ins.then_inc(partsA_ready, 1)

            def edges(l, c, r, k):
                if k == RING:
                    r, k = r + 1, 0
                done = (l * CHUNKS + c) * ROUNDS + r
                dve.wait_ge(adj_landed[k], done * 16 + 16)
                dve.wait_ge(ab_free, done * RING + k + 1)
                tile0 = (r * RING + k) * JG
                for j in range(JG - (k in SIGNED)):
                    ins = nc.vector.tensor_scalar(maskB[:, k, j, :], adj_ring[:, k, j, :], 0.0,
                                                  cA[:, bass.ds(tile0 + j, 1)].bitcast(F32), ALU.is_gt, ALU.mult)
                if k in SIGNED:
                    dve.wait_ge(sign_done, done * len(SIGNED) + SIGNED.index(k) + 1)
                    ins = nc.vector.tensor_scalar(maskB[:, k, JG - 1, :], maskB[:, k, JG - 1, :], 0.0,
                                                  cA[:, bass.ds(tile0 + JG - 1, 1)].bitcast(F32), ALU.max, ALU.mult)
                ins.then_inc(conv_done, 1)

            def group(l, c, r, k, more=True):
                n = ((l * CHUNKS + c) * ROUNDS + r) * RING + k
                dve.wait_ge(relu_done, n + 1)
                dve.wait_ge(conv_done, n + 1)
                nc.vector.tensor_tensor(maskA[:, k, :, :], maskA[:, k, :, :], maskB[:, k, :, :], ALU.min).then_inc(a_made, 1)
                if more:
                    edges(l, c, r, k + 1)
                dve.wait_ge(a_made, n + 1)
                nc.vector.tensor_tensor(maskB[:, k, :, :], maskA[:, k, :, :], maskB[:, k, :, :], ALU.is_lt)\
                  .then_inc(ab_ready, 1)

            def low_sums(n, b):
                dve.wait_ge(hi_added, n * IB + b + 1)
                nc.vector.tensor_tensor(comb[:, b, :], comb[:, b, :], acc[:, b, FD:2 * FD], ALU.add).then_inc(bank_free, 1)

            def evacuate(l, c):
                n = l * CHUNKS + c
                for b in range(IB):
                    dve.wait_ge(b_scaled, n * IB + b + 1)
                    nc.vector.tensor_tensor(comb[:, b, :], comb[:, b, :], acc[:, b, 0:FD], ALU.add).then_inc(hi_added, 1)
                    if b > 0:
                        low_sums(n, b - 1)
                low_sums(n, IB - 1)

            def denominators(l, c):
                n = l * CHUNKS + c
                dve.wait_ge(bank_free, (n + 2) * IB)
                nc.vector.tensor_scalar(no_nb[:, :], comb[:, :, F], 0.0, None, ALU.is_equal).then_inc(no_nb_ready, 1)
                dve.wait_ge(no_nb_ready, n + 1)
                nc.vector.scalar_tensor_tensor(den_q[:, :], comb[:, :, F], qf, no_nb[:, :], ALU.mult, ALU.add)\
                  .then_inc(den_ready, 1)
                dve.wait_ge(den_ready, n + 1)
                nc.vector.reciprocal(inv[:, :], den_q[:, :]).then_inc(inv_ready, 1)

            def finish(l, c):
                n = l * CHUNKS + c
                rows = [flat(X[:, bass.ds(c * IB + b, 1), :]) for b in range(IB)]
                dve.wait_ge(inv_ready, n + 1)
                for b, row in enumerate(rows):
                    ins = nc.vector.scalar_tensor_tensor(row, comb[:, b, 0:F], inv[:, b:b + 1], row, ALU.mult, ALU.add)
                ins.then_inc(attention_added, 1)
                dve.wait_ge(attention_added, l + 1)
                for b, row in enumerate(rows):
                    ins = nc.vector.scalar_tensor_tensor(row, mean_h[:, :], no_nb[:, b:b + 1], row, ALU.mult, ALU.add)
                ins.then_inc(x_done, 1)

            def first_chunk(l):
                def round_(r, low_octet=None, last=False):
                    for k in range(RING):
                        group(l, 0, r, k)
                        if low_octet is not None and k >= 2:
                            low(l, low_octet, k - 2, last)

                group(l, 0, 0, 0, more=False)
                first_lows(l)
                edges(l, 0, 0, 1)
                group(l, 0, 0, 1)
                for k in range(2, RING):
                    group(l, 0, 0, k)
                    low(l, 1, k - 2)
                with dve.Fori(1, ROUNDS - 2) as r:
                    round_(r, r + 1)
                round_(ROUNDS - 2, LAST, last=True)
                round_(ROUNDS - 1)

            def chunk(l, c, last=False):
                for k in range(RING):
                    group(l, c, 0, k)
                    if k == 1:
                        evacuate(l, c - 1)
                denominators(l, c - 1)
                with dve.Fori(1, ROUNDS // 2) as r:
                    for k in range(RING):
                        group(l, c, r, k)
                dve.wait_ge(x_done, settle(dve, l * CHUNKS + c + 1))
                row_moments((l + 1) * CHUNKS + c - 1, (c - 1) * IB)
                if last:
                    roots((l + 1) * 2, (l + 2) * CHUNKS - 1, 0, BEFORE_LAST)
                with dve.Fori(ROUNDS // 2, ROUNDS - last) as r:
                    for k in range(RING):
                        group(l, c, r, k)
                if last:
                    for k in range(RING):
                        group(l, c, ROUNDS - 1, k, more=k < RING - 1)

            dve.sem_inc(partsA_ready, 1)
            dve.sem_inc(x_done, 1)
            dve.sem_inc(quad_free, 2)
            for c in range(CHUNKS - 1):
                dve.wait_ge(x_landed[c], 16)
                row_moments(c, c * IB)
            roots(0, CHUNKS - 1, 0, BEFORE_LAST)
            with dve.Fori(0, LAYERS) as l:
                prepare(l)
                edges(l, 0, 0, 0)
                first_chunk(l)
                with dve.Fori(1, CHUNKS - 1) as c:
                    chunk(l, c)
                chunk(l, CHUNKS - 1, last=True)
                evacuate(l, CHUNKS - 1)
                denominators(l, CHUNKS - 1)
                finish(l, CHUNKS - 1)

    return nc


def kernel(x, adj, L0_gnn_W, L0_gnn_a, L1_gnn_W, L1_gnn_a):
    import numpy as np
    import concourse.bacc as bacc
    from concourse.bass_utils import run_bass_kernel_spmd

    x, adj = np.asarray(x), np.asarray(adj)
    N, F = x.shape
    CW = IB * P
    W = np.stack([np.asarray(L0_gnn_W), np.asarray(L1_gnn_W)])
    a = np.stack([np.asarray(L0_gnn_a), np.asarray(L1_gnn_a)])
    blocks = adj.reshape(N // CW, CW, N // (JG * P), JG, P).transpose(0, 2, 4, 3, 1)
    arrays = {
        "x": np.ascontiguousarray(x),
        "adj": np.ascontiguousarray(blocks).reshape(-1, P, JG * CW),
        "W": np.ascontiguousarray(W),
        "WT": np.ascontiguousarray(W.transpose(0, 2, 1)),
        "a": np.ascontiguousarray(a.reshape(2, 2, F).transpose(0, 2, 1)),
    }
    nc = bacc.Bacc("TRN2", target_bir_lowering=False, num_devices=1)
    args = [nc.dram_tensor(n, v.shape, mybir.dt.from_np(v.dtype), kind="ExternalInput").ap() for n, v in arrays.items()]
    out = nc.dram_tensor("out", x.shape, F32, kind="ExternalOutput").ap()
    gat2_kernel(nc, *args, out)
    r = run_bass_kernel_spmd(nc, [arrays], core_ids=[0])
    return r.results[0]["out"]
```
